# Optimizing a Trainium2 kernel written in Bass

```python
import numpy as np
import jax
import jax.numpy as jnp

def _softmax(x, axis=-1):
    return jax.nn.softmax(x, axis=axis)

def _gelu(x):
    return jax.nn.gelu(x, approximate=True)

def _silu(x):
    return jax.nn.silu(x)

def _sigmoid(x):
    return jax.nn.sigmoid(x)

def _layernorm(x, axis=-1, eps=1e-05):
    m = jnp.mean(x, axis=axis, keepdims=True)
    v = jnp.var(x, axis=axis, keepdims=True)
    return (x - m) / jnp.sqrt(v + eps)

def _scatter_add(tgt, idx, src, axis=0):
    return tgt.at[idx].add(src)

def _segment_sum(src, seg, n):
    return jax.ops.segment_sum(src, seg, n)
kernel_name = 'mk_flamingo_gated_d2_seqx_r8_8a9a1b'

def setup_inputs(seed: int=0):
    np.random.seed(seed)
    _w = jnp.asarray

    def _rec_inputs():
        import jax
        import jax.numpy as jnp
        _rk = jax.random.key(seed)
        x = -0.0003929 + 0.9999 * jax.random.normal(jax.random.fold_in(_rk, 1), (4, 512, 128), jnp.float32)
        _lenS = 512 - jax.random.randint(jax.random.fold_in(_rk, 7), (4,), 0, max(1, 512 // 4) + 1, jnp.int32)
        _lenS2 = 154 - jax.random.randint(jax.random.fold_in(_rk, 8), (4,), 0, max(1, 154 // 4) + 1, jnp.int32)
        _ctx_1024P = jax.random.normal(jax.random.fold_in(_rk, 11), (4, 16, 128), jnp.float32)
        _ctx_1024c = jax.random.dirichlet(jax.random.fold_in(_rk, 511), 0.3 * jnp.ones((16,), jnp.float32), (4, 154))
        _ctx_1024t = jnp.einsum('bsk,bkd->bsd', _ctx_1024c, _ctx_1024P)
        _ctx_1024t = _ctx_1024t * jax.lax.rsqrt(jnp.mean(jnp.square(_ctx_1024t)) + 1e-12) * 0.953939
        ctx_1024 = 2.81802e-05 + 1.00001 * (_ctx_1024t + 0.3 * jax.random.normal(jax.random.fold_in(_rk, 611), (4, 154, 128), jnp.float32))
        _g = jax.random.normal(jax.random.fold_in(_rk, 9001), (2, 2), jnp.float32)
        _g = jnp.sign(_g) * jnp.maximum(jnp.abs(_g), 1.0) + (_g == 0) * 1.0
        g_xattn = _g[0]
        g_ffn = _g[1]
        return (x, ctx_1024, g_xattn, g_ffn)
    x, ctx_1024, g_xattn, g_ffn = _rec_inputs()

    def _L0_xattn_setup():
        import jax, jax.numpy as jnp
        import numpy as np
        key = jax.random.key(seed)
        ks = jax.random.split(key, 9)
        B, S, D = (8, 256, 128)
        Qd = Kd = Vd = 128
        s = 1.0 / np.sqrt(D)
        return {'query': jax.random.normal(ks[0], (B, S, D), jnp.float32), 'key': jax.random.normal(ks[1], (B, S, D), jnp.float32), 'value': jax.random.normal(ks[2], (B, S, D), jnp.float32), 'Wq': jax.random.normal(ks[3], (D, Qd), jnp.float32) * s, 'bq': jnp.zeros((Qd,), jnp.float32), 'Wk': jax.random.normal(ks[4], (D, Kd), jnp.float32) * s, 'bk': jnp.zeros((Kd,), jnp.float32), 'Wv': jax.random.normal(ks[5], (D, Vd), jnp.float32) * s, 'bv': jnp.zeros((Vd,), jnp.float32)}
    _L0_xattn_all = _L0_xattn_setup()
    _L0_xattn_in = {k: v for k, v in _L0_xattn_all.items() if k in ('Wq', 'bq', 'Wk', 'bk', 'Wv', 'bv')}
    del _L0_xattn_all

    def _L0_ffn_setup():
        import jax, jax.numpy as jnp
        import numpy as np
        DIM = 128
        DEPTH = 2
        HEADS = 8
        DIM_HEAD = 64
        WINDOW = 64
        INNER = HEADS * DIM_HEAD
        HID = int(DIM * 4 * 2 / 3)
        B, N = (2, 1024)
        QK_SCALE = 8.0

        def shift_token(t):
            t1, t2 = jnp.split(t, 2, axis=-1)
            t2 = jnp.pad(t2, ((0, 0), (1, 0), (0, 0)))[:, :-1]
            return jnp.concatenate([t1, t2], axis=-1)

        def l2norm(t):
            return t / jnp.clip(jnp.linalg.norm(t, axis=-1, keepdims=True), 1e-12)

        def rotate_half(x):
            x1, x2 = jnp.split(x, 2, axis=-1)
            return jnp.concatenate([-x2, x1], axis=-1)

        def rotary_xpos(q, k):
            n = q.shape[-2]
            half_idx = jnp.arange(0, DIM_HEAD, 2, dtype=jnp.float32)
            inv_freq = 1.0 / 10000.0 ** (half_idx / DIM_HEAD)
            t = jnp.arange(n, dtype=jnp.float32)
            freqs = t[:, None] * inv_freq[None, :]
            freqs = jnp.concatenate([freqs, freqs], axis=-1)
            base = (half_idx + 0.4 * DIM_HEAD) / (1.4 * DIM_HEAD)
            power = (t - n // 2) / float(WINDOW // 2)
            scale = base[None, :] ** power[:, None]
            scale = jnp.concatenate([scale, scale], axis=-1)
            cos, sin = (jnp.cos(freqs), jnp.sin(freqs))
            q = q * cos * scale + rotate_half(q) * sin * scale
            k = k * cos / scale + rotate_half(k) * sin / scale
            return (q, k)

        def local_attention(q, k, v):
            b, h, n, d = q.shape
            w = n // WINDOW
            bq = q.reshape(b, h, w, WINDOW, d) * QK_SCALE
            bk = k.reshape(b, h, w, WINDOW, d)
            bv = v.reshape(b, h, w, WINDOW, d)

            def look_around(t):
                p = jnp.pad(t, ((0, 0), (0, 0), (1, 0), (0, 0), (0, 0)))
                return jnp.concatenate([p[:, :, :w], p[:, :, 1:]], axis=3)
            bk, bv = (look_around(bk), look_around(bv))
            bt = jnp.arange(n).reshape(w, WINDOW)
            btp = jnp.pad(bt, ((1, 0), (0, 0)), constant_values=-1)
            btk = jnp.concatenate([btp[:w], btp[1:]], axis=1)
            sim = jnp.einsum('bhwid,bhwjd->bhwij', bq, bk)
            i = bt[:, :, None]
            j = btk[:, None, :]
            mask = (i < j) | (i > j + WINDOW) | (j == -1)
            sim = jnp.where(mask, -jnp.finfo(sim.dtype).max, sim)
            attn = jax.nn.softmax(sim, axis=-1)
            out = jnp.einsum('bhwij,bhwjd->bhwid', attn, bv)
            return out.reshape(b, h, n, d)

        def _layer(x, wqkv, qs, ksc, wo, lg, lb, w1, b1, w2, b2):
            b, n, _ = x.shape
            h = shift_token(x)
            qkv = h @ wqkv
            q, k, v = jnp.split(qkv, 3, axis=-1)
            to_heads = lambda t: t.reshape(b, n, HEADS, DIM_HEAD).transpose(0, 2, 1, 3)
            q, k, v = (to_heads(q), to_heads(k), to_heads(v))
            q = l2norm(q) * qs
            k = l2norm(k) * ksc
            q, k = rotary_xpos(q, k)
            o = local_attention(q, k, v)
            o = o.transpose(0, 2, 1, 3).reshape(b, n, INNER)
            x = x + o @ wo
            h = shift_token(x)
            mu = h.mean(-1, keepdims=True)
            var = h.var(-1, keepdims=True)
            h = (h - mu) / jnp.sqrt(var + 1e-05) * lg + lb
            h = h @ w1 + b1
            a, g = jnp.split(h, 2, axis=-1)
            h = a * jax.nn.gelu(g, approximate=False)
            x = x + h @ w2 + b2
            return x
        key = jax.random.key(seed)
        ks = jax.random.split(key, 6)
        return {'x': jax.random.normal(ks[0], (B, N, DIM), jnp.float32), 'wqkv': jax.random.normal(ks[1], (DEPTH, DIM, 3 * INNER), jnp.float32) * 0.02, 'q_scale': jnp.ones((DEPTH, DIM_HEAD), jnp.float32), 'k_scale': jnp.ones((DEPTH, DIM_HEAD), jnp.float32), 'wo': jax.random.normal(ks[2], (DEPTH, INNER, DIM), jnp.float32) * 0.02, 'ln_g': jnp.ones((DEPTH, DIM), jnp.float32), 'ln_b': jnp.zeros((DEPTH, DIM), jnp.float32), 'w1': jax.random.normal(ks[3], (DEPTH, DIM, 2 * HID), jnp.float32) * 0.02, 'b1': jnp.zeros((DEPTH, 2 * HID), jnp.float32), 'w2': jax.random.normal(ks[4], (DEPTH, HID, DIM), jnp.float32) * 0.02, 'b2': jnp.zeros((DEPTH, DIM), jnp.float32)}
    _L0_ffn_all = _L0_ffn_setup()
    _L0_ffn_in = {k: v for k, v in _L0_ffn_all.items() if k in ('wqkv', 'q_scale', 'k_scale', 'wo', 'ln_g', 'ln_b', 'w1', 'b1', 'w2', 'b2')}
    del _L0_ffn_all

    def _L1_xattn_setup():
        import jax, jax.numpy as jnp
        import numpy as np
        B, NT, NM, C, H, FF = (8, 128, 256, 128, 8, 512)

        def _ln(x, g, b):
            m = x.mean(-1, keepdims=True)
            v = jnp.mean((x - m) ** 2, axis=-1, keepdims=True)
            return (x - m) / jnp.sqrt(v + 1e-05) * g + b
        key = jax.random.key(seed)
        ks = jax.random.split(key, 8)
        w = lambda k, shape, s=0.02: jax.random.normal(k, shape, dtype=jnp.float32) * s
        return {'tgt': jax.random.normal(ks[0], (B, NT, C), dtype=jnp.float32), 'memory': jax.random.normal(ks[1], (B, NM, C), dtype=jnp.float32), 'qkv_w': w(ks[2], (3 * C, C)), 'qkv_b': jnp.zeros((3 * C,), jnp.float32), 'sa_out_w': w(ks[3], (C, C)), 'sa_out_b': jnp.zeros((C,), jnp.float32), 'in_proj_w': w(ks[4], (3 * C, C)), 'in_proj_b': jnp.zeros((3 * C,), jnp.float32), 'mha_out_w': w(ks[5], (C, C)), 'mha_out_b': jnp.zeros((C,), jnp.float32), 'lin1_w': w(ks[6], (FF, C)), 'lin1_b': jnp.zeros((FF,), jnp.float32), 'lin2_w': w(ks[7], (C, FF)), 'lin2_b': jnp.zeros((C,), jnp.float32), 'ln1_g': jnp.ones((C,), jnp.float32), 'ln1_b': jnp.zeros((C,), jnp.float32), 'ln2_g': jnp.ones((C,), jnp.float32), 'ln2_b': jnp.zeros((C,), jnp.float32), 'ln3_g': jnp.ones((C,), jnp.float32), 'ln3_b': jnp.zeros((C,), jnp.float32)}
    _L1_xattn_all = _L1_xattn_setup()
    _L1_xattn_in = {k: v for k, v in _L1_xattn_all.items() if k in ('qkv_w', 'qkv_b', 'sa_out_w', 'sa_out_b', 'in_proj_w', 'in_proj_b', 'mha_out_w', 'mha_out_b', 'lin1_w', 'lin1_b', 'lin2_w', 'lin2_b', 'ln1_g', 'ln1_b', 'ln2_g', 'ln2_b', 'ln3_g', 'ln3_b')}
    del _L1_xattn_all

    def _L1_ffn_setup():
        import jax, jax.numpy as jnp
        import numpy as np
        B, S, D = (4, 64, 128)
        E, K, H = (64, 8, 32)
        ES, HS = (2, 256)
        key = jax.random.key(seed)
        ks = jax.random.split(key, 8)
        scale = 0.02
        rn = lambda k, shape, s: jax.random.normal(k, shape, jnp.float32) * s
        return {'x': rn(ks[0], (B, S, D), 1.0), 'router_w': rn(ks[1], (D, E), scale), 'router_b': jnp.zeros((E,), jnp.float32), 'w1': rn(ks[2], (E, D, H), scale), 'b1': jnp.zeros((E, H), jnp.float32), 'w2': rn(ks[3], (E, H, D), scale), 'b2': jnp.zeros((E, D), jnp.float32), 'sw1': rn(ks[4], (ES, D, HS), scale), 'sb1': jnp.zeros((ES, HS), jnp.float32), 'sw2': rn(ks[5], (ES, HS, D), scale), 'sb2': jnp.zeros((ES, D), jnp.float32)}
    _L1_ffn_all = _L1_ffn_setup()
    _L1_ffn_in = {k: v for k, v in _L1_ffn_all.items() if k in ('router_w', 'router_b', 'w1', 'b1', 'w2', 'b2', 'sw1', 'sb1', 'sw2', 'sb2')}
    del _L1_ffn_all
    return {'x': x, 'ctx_1024': ctx_1024, 'g_xattn': g_xattn, 'g_ffn': g_ffn, 'L0_xattn_Wq': _L0_xattn_in['Wq'], 'L0_xattn_bq': _L0_xattn_in['bq'], 'L0_xattn_Wk': _L0_xattn_in['Wk'], 'L0_xattn_bk': _L0_xattn_in['bk'], 'L0_xattn_Wv': _L0_xattn_in['Wv'], 'L0_xattn_bv': _L0_xattn_in['bv'], 'L0_ffn_wqkv': _L0_ffn_in['wqkv'], 'L0_ffn_q_scale': _L0_ffn_in['q_scale'], 'L0_ffn_k_scale': _L0_ffn_in['k_scale'], 'L0_ffn_wo': _L0_ffn_in['wo'], 'L0_ffn_ln_g': _L0_ffn_in['ln_g'], 'L0_ffn_ln_b': _L0_ffn_in['ln_b'], 'L0_ffn_w1': _L0_ffn_in['w1'], 'L0_ffn_b1': _L0_ffn_in['b1'], 'L0_ffn_w2': _L0_ffn_in['w2'], 'L0_ffn_b2': _L0_ffn_in['b2'], 'L1_xattn_qkv_w': _L1_xattn_in['qkv_w'], 'L1_xattn_qkv_b': _L1_xattn_in['qkv_b'], 'L1_xattn_sa_out_w': _L1_xattn_in['sa_out_w'], 'L1_xattn_sa_out_b': _L1_xattn_in['sa_out_b'], 'L1_xattn_in_proj_w': _L1_xattn_in['in_proj_w'], 'L1_xattn_in_proj_b': _L1_xattn_in['in_proj_b'], 'L1_xattn_mha_out_w': _L1_xattn_in['mha_out_w'], 'L1_xattn_mha_out_b': _L1_xattn_in['mha_out_b'], 'L1_xattn_lin1_w': _L1_xattn_in['lin1_w'], 'L1_xattn_lin1_b': _L1_xattn_in['lin1_b'], 'L1_xattn_lin2_w': _L1_xattn_in['lin2_w'], 'L1_xattn_lin2_b': _L1_xattn_in['lin2_b'], 'L1_xattn_ln1_g': _L1_xattn_in['ln1_g'], 'L1_xattn_ln1_b': _L1_xattn_in['ln1_b'], 'L1_xattn_ln2_g': _L1_xattn_in['ln2_g'], 'L1_xattn_ln2_b': _L1_xattn_in['ln2_b'], 'L1_xattn_ln3_g': _L1_xattn_in['ln3_g'], 'L1_xattn_ln3_b': _L1_xattn_in['ln3_b'], 'L1_ffn_router_w': _L1_ffn_in['router_w'], 'L1_ffn_router_b': _L1_ffn_in['router_b'], 'L1_ffn_w1': _L1_ffn_in['w1'], 'L1_ffn_b1': _L1_ffn_in['b1'], 'L1_ffn_w2': _L1_ffn_in['w2'], 'L1_ffn_b2': _L1_ffn_in['b2'], 'L1_ffn_sw1': _L1_ffn_in['sw1'], 'L1_ffn_sb1': _L1_ffn_in['sb1'], 'L1_ffn_sw2': _L1_ffn_in['sw2'], 'L1_ffn_sb2': _L1_ffn_in['sb2']}

def reference(x, ctx_1024, g_xattn, g_ffn, L0_xattn_Wq, L0_xattn_bq, L0_xattn_Wk, L0_xattn_bk, L0_xattn_Wv, L0_xattn_bv, L0_ffn_wqkv, L0_ffn_q_scale, L0_ffn_k_scale, L0_ffn_wo, L0_ffn_ln_g, L0_ffn_ln_b, L0_ffn_w1, L0_ffn_b1, L0_ffn_w2, L0_ffn_b2, L1_xattn_qkv_w, L1_xattn_qkv_b, L1_xattn_sa_out_w, L1_xattn_sa_out_b, L1_xattn_in_proj_w, L1_xattn_in_proj_b, L1_xattn_mha_out_w, L1_xattn_mha_out_b, L1_xattn_lin1_w, L1_xattn_lin1_b, L1_xattn_lin2_w, L1_xattn_lin2_b, L1_xattn_ln1_g, L1_xattn_ln1_b, L1_xattn_ln2_g, L1_xattn_ln2_b, L1_xattn_ln3_g, L1_xattn_ln3_b, L1_ffn_router_w, L1_ffn_router_b, L1_ffn_w1, L1_ffn_b1, L1_ffn_w2, L1_ffn_b2, L1_ffn_sw1, L1_ffn_sb1, L1_ffn_sw2, L1_ffn_sb2):
    import jax
    import jax.numpy as jnp

    def _L0_xattn_ref(query, key, value, Wq, bq, Wk, bk, Wv, bv):
        import jax, jax.numpy as jnp
        import numpy as np
        Q = jnp.einsum('bsd,de->bse', query, Wq) + bq
        K = jnp.einsum('bsd,de->bse', key, Wk) + bk
        V = jnp.einsum('bsd,de->bse', value, Wv) + bv
        scale = 1.0 / jnp.sqrt(jnp.asarray(K.shape[-1], Q.dtype))
        scores = jnp.einsum('bqe,bke->bqk', Q, K) * scale
        attn = jax.nn.softmax(scores, axis=-1)
        return jnp.einsum('bqk,bkv->bqv', attn, V)

    def _L0_ffn_ref(x, wqkv, q_scale, k_scale, wo, ln_g, ln_b, w1, b1, w2, b2):
        import jax, jax.numpy as jnp
        import numpy as np
        DIM = 128
        DEPTH = 2
        HEADS = 8
        DIM_HEAD = 64
        WINDOW = 64
        INNER = HEADS * DIM_HEAD
        HID = int(DIM * 4 * 2 / 3)
        B, N = (2, 1024)
        QK_SCALE = 8.0

        def shift_token(t):
            t1, t2 = jnp.split(t, 2, axis=-1)
            t2 = jnp.pad(t2, ((0, 0), (1, 0), (0, 0)))[:, :-1]
            return jnp.concatenate([t1, t2], axis=-1)

        def l2norm(t):
            return t / jnp.clip(jnp.linalg.norm(t, axis=-1, keepdims=True), 1e-12)

        def rotate_half(x):
            x1, x2 = jnp.split(x, 2, axis=-1)
            return jnp.concatenate([-x2, x1], axis=-1)

        def rotary_xpos(q, k):
            n = q.shape[-2]
            half_idx = jnp.arange(0, DIM_HEAD, 2, dtype=jnp.float32)
            inv_freq = 1.0 / 10000.0 ** (half_idx / DIM_HEAD)
            t = jnp.arange(n, dtype=jnp.float32)
            freqs = t[:, None] * inv_freq[None, :]
            freqs = jnp.concatenate([freqs, freqs], axis=-1)
            base = (half_idx + 0.4 * DIM_HEAD) / (1.4 * DIM_HEAD)
            power = (t - n // 2) / float(WINDOW // 2)
            scale = base[None, :] ** power[:, None]
            scale = jnp.concatenate([scale, scale], axis=-1)
            cos, sin = (jnp.cos(freqs), jnp.sin(freqs))
            q = q * cos * scale + rotate_half(q) * sin * scale
            k = k * cos / scale + rotate_half(k) * sin / scale
            return (q, k)

        def local_attention(q, k, v):
            b, h, n, d = q.shape
            w = n // WINDOW
            bq = q.reshape(b, h, w, WINDOW, d) * QK_SCALE
            bk = k.reshape(b, h, w, WINDOW, d)
            bv = v.reshape(b, h, w, WINDOW, d)

            def look_around(t):
                p = jnp.pad(t, ((0, 0), (0, 0), (1, 0), (0, 0), (0, 0)))
                return jnp.concatenate([p[:, :, :w], p[:, :, 1:]], axis=3)
            bk, bv = (look_around(bk), look_around(bv))
            bt = jnp.arange(n).reshape(w, WINDOW)
            btp = jnp.pad(bt, ((1, 0), (0, 0)), constant_values=-1)
            btk = jnp.concatenate([btp[:w], btp[1:]], axis=1)
            sim = jnp.einsum('bhwid,bhwjd->bhwij', bq, bk)
            i = bt[:, :, None]
            j = btk[:, None, :]
            mask = (i < j) | (i > j + WINDOW) | (j == -1)
            sim = jnp.where(mask, -jnp.finfo(sim.dtype).max, sim)
            attn = jax.nn.softmax(sim, axis=-1)
            out = jnp.einsum('bhwij,bhwjd->bhwid', attn, bv)
            return out.reshape(b, h, n, d)

        def _layer(x, wqkv, qs, ksc, wo, lg, lb, w1, b1, w2, b2):
            b, n, _ = x.shape
            h = shift_token(x)
            qkv = h @ wqkv
            q, k, v = jnp.split(qkv, 3, axis=-1)
            to_heads = lambda t: t.reshape(b, n, HEADS, DIM_HEAD).transpose(0, 2, 1, 3)
            q, k, v = (to_heads(q), to_heads(k), to_heads(v))
            q = l2norm(q) * qs
            k = l2norm(k) * ksc
            q, k = rotary_xpos(q, k)
            o = local_attention(q, k, v)
            o = o.transpose(0, 2, 1, 3).reshape(b, n, INNER)
            x = x + o @ wo
            h = shift_token(x)
            mu = h.mean(-1, keepdims=True)
            var = h.var(-1, keepdims=True)
            h = (h - mu) / jnp.sqrt(var + 1e-05) * lg + lb
            h = h @ w1 + b1
            a, g = jnp.split(h, 2, axis=-1)
            h = a * jax.nn.gelu(g, approximate=False)
            x = x + h @ w2 + b2
            return x
        for l in range(DEPTH):
            x = _layer(x, wqkv[l], q_scale[l], k_scale[l], wo[l], ln_g[l], ln_b[l], w1[l], b1[l], w2[l], b2[l])
        return x

    def _L1_xattn_ref(tgt, memory, qkv_w, qkv_b, sa_out_w, sa_out_b, in_proj_w, in_proj_b, mha_out_w, mha_out_b, lin1_w, lin1_b, lin2_w, lin2_b, ln1_g, ln1_b, ln2_g, ln2_b, ln3_g, ln3_b):
        import jax, jax.numpy as jnp
        import numpy as np
        B, NT, NM, C, H, FF = (8, 128, 256, 128, 8, 512)

        def _ln(x, g, b):
            m = x.mean(-1, keepdims=True)
            v = jnp.mean((x - m) ** 2, axis=-1, keepdims=True)
            return (x - m) / jnp.sqrt(v + 1e-05) * g + b
        Bx, N, Cx = tgt.shape
        qkv = tgt @ qkv_w.T + qkv_b
        q, k, v = jnp.split(qkv, 3, axis=-1)
        scores = jnp.einsum('bnc,bmc->bnm', q, k) * jnp.sqrt(jnp.float32(Cx))
        diag = jnp.eye(N, dtype=bool)
        scores = jnp.where(diag[None, :, :], scores, -jnp.inf)
        attn = jax.nn.softmax(scores, axis=-1)
        sa = jnp.einsum('bnm,bmc->bnc', attn, v) @ sa_out_w.T + sa_out_b
        x = _ln(tgt + sa, ln1_g, ln1_b)
        d = Cx // H
        wq, wk, wv = jnp.split(in_proj_w, 3, axis=0)
        bq, bk, bv = jnp.split(in_proj_b, 3, axis=0)
        qh = (x @ wq.T + bq).reshape(Bx, N, H, d).transpose(0, 2, 1, 3)
        kh = (memory @ wk.T + bk).reshape(Bx, -1, H, d).transpose(0, 2, 1, 3)
        vh = (memory @ wv.T + bv).reshape(Bx, -1, H, d).transpose(0, 2, 1, 3)
        a = jax.nn.softmax(jnp.einsum('bhnd,bhmd->bhnm', qh, kh) / jnp.sqrt(jnp.float32(d)), axis=-1)
        ca = jnp.einsum('bhnm,bhmd->bhnd', a, vh).transpose(0, 2, 1, 3).reshape(Bx, N, Cx)
        ca = ca @ mha_out_w.T + mha_out_b
        x = _ln(x + ca, ln2_g, ln2_b)
        ff = jax.nn.relu(x @ lin1_w.T + lin1_b) @ lin2_w.T + lin2_b
        return _ln(x + ff, ln3_g, ln3_b)

    def _L1_ffn_ref(x, router_w, router_b, w1, b1, w2, b2, sw1, sb1, sw2, sb2):
        import jax, jax.numpy as jnp
        import numpy as np
        B, S, D = (4, 64, 128)
        E, K, H = (64, 8, 32)
        ES, HS = (2, 256)
        b_, s_, d_ = x.shape
        xf = x.reshape(-1, d_)
        probs = jax.nn.softmax(xf @ router_w + router_b, axis=-1)
        tw, ti = jax.lax.top_k(probs, K)
        tw = tw / jnp.sum(tw, axis=-1, keepdims=True)

        def body(acc, p):
            W1, B1, W2, B2, e = p
            h = jax.nn.silu(xf @ W1 + B1) @ W2 + B2
            cw = jnp.sum(jnp.where(ti == e, tw, 0.0), axis=-1)
            return (acc + cw[:, None] * h, None)
        routed, _ = jax.lax.scan(body, jnp.zeros_like(xf), (w1, b1, w2, b2, jnp.arange(w1.shape[0])))

        def shared_mlp(W1, B1, W2, B2):
            return jax.nn.silu(xf @ W1 + B1) @ W2 + B2
        shared = jnp.sum(jax.vmap(shared_mlp)(sw1, sb1, sw2, sb2), axis=0)
        return (routed + shared).reshape(b_, s_, d_)
    x = x + jnp.tanh(g_xattn[0]) * _L0_xattn_ref(_layernorm(x, axis=-1), ctx_1024, ctx_1024, L0_xattn_Wq, L0_xattn_bq, L0_xattn_Wk, L0_xattn_bk, L0_xattn_Wv, L0_xattn_bv)
    x = x + jnp.tanh(g_ffn[0]) * _L0_ffn_ref(_layernorm(x, axis=-1), L0_ffn_wqkv, L0_ffn_q_scale, L0_ffn_k_scale, L0_ffn_wo, L0_ffn_ln_g, L0_ffn_ln_b, L0_ffn_w1, L0_ffn_b1, L0_ffn_w2, L0_ffn_b2)
    x = x + jnp.tanh(g_xattn[1]) * _L1_xattn_ref(_layernorm(x, axis=-1), ctx_1024, L1_xattn_qkv_w, L1_xattn_qkv_b, L1_xattn_sa_out_w, L1_xattn_sa_out_b, L1_xattn_in_proj_w, L1_xattn_in_proj_b, L1_xattn_mha_out_w, L1_xattn_mha_out_b, L1_xattn_lin1_w, L1_xattn_lin1_b, L1_xattn_lin2_w, L1_xattn_lin2_b, L1_xattn_ln1_g, L1_xattn_ln1_b, L1_xattn_ln2_g, L1_xattn_ln2_b, L1_xattn_ln3_g, L1_xattn_ln3_b)
    x = x + jnp.tanh(g_ffn[1]) * _L1_ffn_ref(_layernorm(x, axis=-1), L1_ffn_router_w, L1_ffn_router_b, L1_ffn_w1, L1_ffn_b1, L1_ffn_w2, L1_ffn_b2, L1_ffn_sw1, L1_ffn_sb1, L1_ffn_sw2, L1_ffn_sb2)
    return x

_drawn_inputs = setup_inputs


def setup_inputs(seed=0):
    import zlib

    import numpy as np

    out = dict(_drawn_inputs(seed))
    spreads = {'g_ffn': (-1.0, 0.6),
     'L0_xattn_bq': (0.0, 0.433),
     'L0_xattn_bk': (0.0, 0.8),
     'L0_xattn_bv': (0.0, 0.1),
     'L0_ffn_q_scale': (1.0, 0.6),
     'L0_ffn_k_scale': (1.0, 0.6),
     'L0_ffn_ln_g': (1.0, 0.6),
     'L0_ffn_ln_b': (0.0, 0.8),
     'L0_ffn_b1': (0.0, 0.364),
     'L0_ffn_b2': (0.0, 0.1),
     'L1_xattn_qkv_b': (0.0, 0.1),
     'L1_xattn_sa_out_b': (0.0, 0.1),
     'L1_xattn_in_proj_b': (0.0, 0.1),
     'L1_xattn_mha_out_b': (0.0, 0.1),
     'L1_xattn_lin1_b': (0.0, 0.1),
     'L1_xattn_lin2_b': (0.0, 0.1),
     'L1_xattn_ln1_g': (1.0, 0.2),
     'L1_xattn_ln1_b': (0.0, 0.1),
     'L1_xattn_ln2_g': (1.0, 0.2),
     'L1_xattn_ln2_b': (0.0, 0.1),
     'L1_xattn_ln3_g': (1.0, 0.2),
     'L1_xattn_ln3_b': (0.0, 0.1),
     'L1_ffn_router_b': (0.0, 0.1),
     'L1_ffn_b1': (0.0, 0.8),
     'L1_ffn_b2': (0.0, 0.1),
     'L1_ffn_sb1': (0.0, 0.286),
     'L1_ffn_sb2': (0.0, 0.1)}
    factors = {'L1_ffn_w1': 8.0, 'L1_ffn_w2': 8.0}
    for name, (base, spread) in spreads.items():
        noise = np.random.default_rng([zlib.crc32(name.encode()), seed]).standard_normal(out[name].shape)
        drawn = base * np.exp(spread * noise) if base else spread * noise
        out[name] = jnp.asarray(drawn.astype(out[name].dtype))
    for name, factor in factors.items():
        out[name] = (out[name] * factor).astype(out[name].dtype)
    return out
```

```python
from contextlib import ExitStack

import numpy as np

import concourse.bass as bass
from concourse import mybir

ALU = mybir.AluOpType
ACT = mybir.ActivationFunctionType
AX = mybir.AxisListType
F32 = mybir.dt.float32
BF16 = mybir.dt.bfloat16

BATCH, SEQ, D = 4, 512, 128
P = 128
TILES = SEQ // P
SLOTS = (0, 1)
CTX = 154
CH = CTX // 2
LAYERS, HEADS, DH, WINDOW = 2, 8, 64, 64
INNER = HEADS * DH
KEYS = P + WINDOW
HID = int(D * 4 * 2 / 3)
HID_W = [min(P, HID - m * P) for m in range(-(-HID // P))]
CA_HEADS, CA_DH = 8, 16
FF = 512
EXPERTS, TOPK, EXP_H = 64, 8, 32
ROUTED = EXPERTS * EXP_H // P
SHARED = 4
EPS = 1e-5
MASKED = -1.0e30
LOWEST = -3.0e38
ACT_BANKS, DVE_BANKS = 3, 4

LN_XATTN, LN_OUTER, LN_FF, LN_TGT, LN_1, LN_2, LN_3, LN_MOE = 0, 1, (2, 3), 4, 5, 6, 7, 8
SM_FIRST = 0


def sm_local(l, t):
    return 1 + TILES * l + t


def sm_cross(t):
    return 1 + TILES * LAYERS + t


def layout(names):
    at, out = 0, {}
    for name, w in names:
        out[name] = (at, w)
        at += w
    return out, at


COLS, N_COLS = layout([
    ("bq", 1), ("bk", 1), ("ln_g", 2), ("ln_b", 2), ("b1a", 6), ("b1g", 6), ("bv_sa", 1),
    ("ln1_g", 1), ("ln1_b", 1), ("ln2_g", 1), ("ln2_b", 1), ("bq_ca", 2), ("bk_ca", 2),
    ("lin1_b", 4), ("moe_b1", ROUTED), ("sb1", SHARED), ("sb2", 2)])
ROWS, N_ROWS = layout([
    ("gates", 4), ("bv", D), ("qs", 2 * DH), ("ks", 2 * DH), ("qs_swap", 2 * DH), ("ks_swap", 2 * DH),
    ("b2", 2 * D), ("bqk_sa", 2 * D), ("sa_out_b", D), ("ln1_g", D), ("ln1_b", D), ("mha_out_b", D),
    ("ln2_g", D), ("ln2_b", D), ("lin2_b", D), ("ln3_g", D), ("ln3_b", D), ("bv_ca", D),
    ("router_b", EXPERTS)])
GX0, GX1, GF0, GF1 = range(4)


def rotary_tables():
    f = np.float32
    half = np.arange(0, DH, 2, dtype=f)
    inv_freq = (f(1.0) / np.power(f(10000.0), half / f(DH))).astype(f)
    t = np.arange(SEQ, dtype=f)
    freqs = (t[:, None] * inv_freq[None, :]).astype(f)
    base = ((half + f(0.4 * DH)) / f(1.4 * DH)).astype(f)
    power = ((t - f(SEQ // 2)) / f(WINDOW // 2)).astype(f)
    scale = np.power(base[None, :], power[:, None]).astype(f)
    cos, sin = np.cos(freqs), np.sin(freqs)
    a = np.stack([np.concatenate([cos * scale] * 2, -1), np.concatenate([cos / scale] * 2, -1)], 1)
    b = np.stack([np.concatenate([-sin * scale, sin * scale], -1),
                  np.concatenate([-sin / scale, sin / scale], -1)], 1)
    shape = (TILES, P, 2, DH)
    return [np.ascontiguousarray(x.astype(f).reshape(shape).transpose(1, 0, 2, 3).reshape(P, -1)) for x in (a, b)]


def band_masks():
    i = np.arange(P)[:, None]
    j = np.arange(KEYS)[None, :] - WINDOW
    band = np.where((j <= i) & (j >= i - WINDOW), 0.0, MASKED)
    first = np.where(j < 0, MASKED, band)
    return np.stack([first, band], 1).reshape(P, 2 * KEYS).astype(np.float32)


def expert_selector():
    sel = np.zeros((EXPERTS, ROUTED, P), np.float32)
    for c in range(ROUTED):
        for j in range(P):
            sel[c * (P // EXP_H) + j // EXP_H, c, j] = 1.0
    return np.concatenate([sel, sel], 0).reshape(2 * EXPERTS, ROUTED * P)


def build(nc, a, out):
    ctx = ExitStack()
    with ctx:
        def sb(name, shape, dt=F32):
            return ctx.enter_context(nc.sbuf_tensor(name, shape, dt))

        def per_slot(name, shape, dt=F32):
            return [sb(f"{name}{u}", shape, dt) for u in SLOTS]

        def sem(name):
            return ctx.enter_context(nc.semaphore(name))

        cols = sb("cols", [P, N_COLS])
        rows = sb("rows", [P, N_ROWS])
        ident = sb("ident", [P, P])
        identb = sb("identb", [P, P], BF16)
        masks = sb("masks", [P, 2, KEYS])
        no_mask = sb("no_mask", [P, CTX])
        sel = sb("sel", [P, ROUTED, P], BF16)
        ones_row = sb("ones_row", [1, P])
        neg_half = sb("neg_half", [P, 2 * HEADS])
        gate = sb("gate", [P, 4])
        wq, wk, wv = (sb(n, [P, D]) for n in ("wq", "wk", "wv"))
        wqkv = sb("wqkv", [P, LAYERS, 3 * INNER])
        wo = sb("wo", [P, LAYERS, INNER // P, D])
        w1 = sb("w1", [P, LAYERS, 2 * HID])
        w2 = sb("w2", [P, LAYERS, len(HID_W), D])
        w_sa = sb("w_sa", [P, 3 * D])
        w_sao = sb("w_sao", [P, D])
        w_caq = sb("w_caq", [P, 2, P])
        w_cak = sb("w_cak", [P, 2, P])
        w_cav = sb("w_cav", [P, D])
        w_cao = sb("w_cao", [P, D])
        w_l1 = sb("w_l1", [P, FF])
        w_l2 = sb("w_l2", [P, FF // P, D])
        w_rt = sb("w_rt", [P, EXPERTS])
        w_m1 = sb("w_m1", [P, ROUTED * P])
        w_m2 = sb("w_m2", [P, ROUTED, D])
        w_s1 = sb("w_s1", [P, SHARED, P])
        w_s2 = sb("w_s2", [P, SHARED, D])
        b_m2 = sb("b_m2", [EXPERTS, D])
        tab_a = sb("tab_a", [P, LAYERS, TILES, 2, DH])
        tab_b = sb("tab_b", [P, LAYERS, TILES, 2, DH])
        res1_b = sb("res1_b", [P, D])
        res2_b = sb("res2_b", [P, D])
        g3 = sb("g3", [P, D])
        b3 = sb("b3", [P, D])
        sb2_sum = sb("sb2_sum", [P, 1])
        sb2_g = sb("sb2_g", [P, 1])

        x = per_slot("x", [P, TILES, D])
        y = per_slot("y", [P, TILES, D])
        res = per_slot("res", [P, TILES, D])
        nrm = per_slot("nrm", [P, TILES, D])
        shifted = per_slot("shifted", [P, TILES, D])
        stats = per_slot("stats", [P, TILES, 6])
        mv = per_slot("mv", [P, TILES, 2])
        rstd = per_slot("rstd", [P, TILES])
        ctx_t = per_slot("ctx_t", [CH, 2, D])
        ctxT = per_slot("ctxT", [P, CTX])
        hT = per_slot("hT", [P, SEQ])
        hTs = per_slot("hTs", [P, WINDOW + SEQ])
        qT = per_slot("qT", [P, INNER // P, SEQ])
        kT = per_slot("kT", [P, INNER // P, WINDOW + SEQ])
        kcT = per_slot("kcT", [P, 2, CTX])
        v_loc = per_slot("v_loc", [P, TILES + 1, INNER])
        v_ctx = per_slot("v_ctx", [CH, 2, D])
        work = per_slot("work", [P, 3 * 2 * INNER])
        ptb = per_slot("ptb", [P, HEADS, P])
        oT = [h[:].rearrange("p (c q) -> p c q", q=P) for h in hT]
        peak = per_slot("peak", [P, HEADS])
        nbias = per_slot("nbias", [P, HEADS])
        sums = per_slot("sums", [P, HEADS])
        rinv = per_slot("rinv", [P, HEADS])
        sumsq = per_slot("sumsq", [P, TILES, 2 * HEADS])
        rnorm = per_slot("rnorm", [P, TILES, 2 * HEADS])
        diag = per_slot("diag", [P, 4, TILES])
        W2 = 2 * INNER
        rot_a, rot_b = (work[0][:, k * 512:(k + 1) * 512].rearrange("p (t a d) -> p t a d", t=TILES, a=2) for k in range(2))
        raw = [w[:, 0:W2].rearrange("p (a n) -> p a n", a=2) for w in work]
        partner = [w[:, W2:2 * W2].rearrange("p (a n) -> p a n", a=2) for w in work]
        turned = [w[:, 2 * W2:3 * W2].rearrange("p (a n) -> p a n", a=2) for w in work]
        prob = [w[:, 0:HEADS * KEYS].rearrange("p (h k) -> p h k", h=HEADS) for w in work]
        pta = [w[:, 1536:2560].rearrange("p (h q) -> p h q", h=HEADS) for w in work]
        otok = [w[:, 2560:3072] for w in work]
        gel = [w[:, 0:3 * SEQ].rearrange("p (m n) -> p m n", m=3) for w in work]
        hid = [w[:, 0:3 * SEQ].rearrange("p (m n) -> p m n", m=3) for w in work]
        weighed = [w[:, 3 * SEQ:6 * SEQ].rearrange("p (m n) -> p m n", m=3) for w in work]
        def route_view(u, k, n):
            return v_loc[u][:, k, 0:n]
        logit = [route_view(u, 0, 256).rearrange("p (t e) -> p t e", t=TILES) for u in SLOTS]
        expw = [route_view(u, 1, 256).rearrange("p (t e) -> p t e", t=TILES) for u in SLOTS]
        rest = [route_view(u, 2, 256).rearrange("p (t e) -> p t e", t=TILES) for u in SLOTS]
        cw = [route_view(u, 3, 256).rearrange("p (t e) -> p t e", t=TILES) for u in SLOTS]
        cwT = [v_loc[u][0:EXPERTS, 4, :] for u in SLOTS]
        top = per_slot("top", [P, TILES, TOPK])
        rsmall = per_slot("rsmall", [P, 3, TILES])
        cw_hm = [v_loc[u][:, 0, 256:512].bitcast(BF16).rearrange("p (t e) -> p t e", t=TILES) for u in SLOTS]
        cw_lo = [v_loc[u][:, 1, 256:384].bitcast(BF16).rearrange("p (t e) -> p t e", t=TILES) for u in SLOTS]
        cwT_hm = [v_loc[u][:, 2, 256:512].bitcast(BF16) for u in SLOTS]
        cwT_lo = [v_loc[u][0:EXPERTS, 3, 256:512].bitcast(BF16) for u in SLOTS]

        def flat(t):
            return t[:].rearrange("p t d -> p (t d)")

        def col(name, k=0, n=P):
            at, _ = COLS[name]
            return cols[0:n, at + k:at + k + 1]

        def row(name, k=0, w=D, n=P):
            at, _ = ROWS[name]
            return rows[0:n, at + k * w:at + k * w + w]

        act_psum = [ctx.enter_context(nc.psum_tensor(f"act_psum{i}", [P, 512], F32)) for i in range(ACT_BANKS)]
        dve_psum = [ctx.enter_context(nc.psum_tensor(f"dve_psum{i}", [P, 512], F32)) for i in range(DVE_BANKS)]
        moe_psum = ctx.enter_context(nc.psum_tensor("moe_psum", [P, 512], F32))

        small_loaded = sem("small_loaded")
        w_loaded = {k: sem(f"{k}_loaded") for k in ("first", "local", "cross", "moe")}
        set_up = sem("set_up")
        gate_made = sem("gate_made")
        pool_setup = sem("pool_setup")

        loop_sem_numbers = []

        def loop_sem(name):
            s = sem(name)
            loop_sem_numbers.append(s.num)
            return s

        def slot_sems(name):
            return [loop_sem(f"{name}{u}") for u in SLOTS]

        act_filled, act_emptied = loop_sem("act_filled"), loop_sem("act_emptied")
        dve_filled, dve_emptied = loop_sem("dve_filled"), loop_sem("dve_emptied")
        act_chain, dve_chain, pool_chain = loop_sem("act_chain"), loop_sem("dve_chain"), loop_sem("pool_chain")
        x_loaded, ctx_loaded = slot_sems("x_loaded"), slot_sems("ctx_loaded")
        ln_stats, ln_rstd, ln_done = slot_sems("ln_stats"), slot_sems("ln_rstd"), slot_sems("ln_done")
        peak_ready, exp_done = slot_sems("peak_ready"), slot_sems("exp_done")
        sq_ready, sumsq_ready, rnorm_ready = slot_sems("sq_ready"), slot_sems("sumsq_ready"), slot_sems("rnorm_ready")
        partner_ready, turned_ready, k_ready = slot_sems("partner_ready"), slot_sems("turned_ready"), slot_sems("k_ready")
        own_ready, rinv_ready = slot_sems("own_ready"), slot_sems("rinv_ready")
        res_ready, shift_done = slot_sems("res_ready"), slot_sems("shift_done")
        diag_ready, diag_exp = slot_sems("diag_ready"), slot_sems("diag_exp")
        logit_ready, expw_ready, cw_ready = slot_sems("logit_ready"), slot_sems("expw_ready"), slot_sems("cw_ready")
        moe_filled, moe_emptied = loop_sem("moe_filled"), loop_sem("moe_emptied")
        x_stored = slot_sems("x_stored")

        with nc.Block() as block:
            @block.sync
            def _(sp):
                for dst, src in ((rows[:], a["rows"].to_broadcast([P, N_ROWS])), (cols[:], a["cols"]), (ident[:], a["ident"]),
                                 (work[0][:, 0:512], a["rot_a"]), (work[0][:, 512:1024], a["rot_b"]),
                                 (masks[:].rearrange("p m k -> p (m k)"), a["masks"]), (sel[:].rearrange("p c n -> p (c n)"), a["sel"]), (identb[:], a["identb"])):
                    sp.dma_start(dst, src).then_inc(small_loaded, 16)
                for dst, src in ((wk[:], a["wk"]), (wv[:], a["wv"]), (wq[:], a["wq"])):
                    sp.dma_start(dst, src).then_inc(w_loaded["first"], 16)
                sp.dma_start(wqkv[:], a["wqkv"].rearrange("l p n -> p l n")).then_inc(w_loaded["local"], 16)
                sp.dma_start(wo[:].rearrange("p l c n -> p (l c) n"),
                             a["wo"].rearrange("l (c p) n -> p (l c) n", p=P)).then_inc(w_loaded["local"], 16)
                sp.dma_start(w1[:], a["w1"].rearrange("l p n -> p l n")).then_inc(w_loaded["local"], 16)
                for m, w in enumerate(HID_W):
                    sp.dma_start(w2[0:w, :, m, :], a["w2"][:, m * P:m * P + w, :].rearrange("l p n -> p l n"))\
                      .then_inc(w_loaded["local"], 16)
                for dst, src in ((w_sa[:], a["w_sa"]), (w_sao[:], a["w_sao"]),
                                 (w_caq[:].rearrange("p c n -> p (c n)"), a["w_caq"]),
                                 (w_cak[:].rearrange("p c n -> p (c n)"), a["w_cak"]),
                                 (w_cav[:], a["w_cav"]), (w_cao[:], a["w_cao"]), (w_l1[:], a["w_l1"]),
                                 (w_l2[:], a["w_l2"].rearrange("(c p) n -> p c n", p=P))):
                    sp.dma_start(dst, src).then_inc(w_loaded["cross"], 16)
                for dst, src in ((w_rt[:], a["w_rt"]), (b_m2[:], a["b_m2"]), (w_m1[:], a["w_m1"]),
                                 (w_m2[:], a["w_m2"].rearrange("(c p) n -> p c n", p=P)),
                                 (w_s1[:].rearrange("p (e c) n -> p e (c n)", e=2), a["w_s1"].rearrange("e p n -> p e n")),
                                 (w_s2[:].rearrange("p (e c) n -> p e c n", e=2),
                                  a["w_s2"].rearrange("e (c p) n -> p e c n", p=P))):
                    sp.dma_start(dst, src).then_inc(w_loaded["moe"], 16)

            @block.scalar
            def _(act):
                act.wait_ge(small_loaded, 8 * 16)
                at, _ = ROWS["gates"]
                nc.scalar.activation(gate[:], rows[:, at:at + 4], ACT.Tanh).then_inc(gate_made, 1)

            @block.vector
            def _(dve):
                nc.vector.memset(no_mask[:], 0.0)
                nc.vector.memset(ones_row[:], 1.0)
                nc.vector.memset(neg_half[:], -0.5)
                for u in SLOTS:
                    nc.vector.memset(hTs[u][:, 0:WINDOW], 0.0)
                    nc.vector.memset(hTs[u][D // 2:D, WINDOW:WINDOW + 1], 0.0)
                    nc.vector.memset(kT[u][:, :, 0:WINDOW], 0.0)
                    nc.vector.memset(shifted[u][0:1, 0, D // 2:D], 0.0)
                dve.wait_ge(small_loaded, 8 * 16)
                nc.vector.tensor_tensor(res1_b[:], row("ln1_b"), row("mha_out_b"), ALU.add)
                nc.vector.tensor_tensor(res2_b[:], row("ln2_b"), row("lin2_b"), ALU.add)
                nc.vector.tensor_tensor(sb2_sum[:], col("sb2", 0), col("sb2", 1), ALU.add).then_inc(set_up, 1)
                dve.wait_ge(gate_made, 1)
                nc.vector.tensor_scalar(g3[:], row("ln3_g"), gate[:, GX1:GX1 + 1], None, ALU.mult)
                nc.vector.tensor_scalar(b3[:], row("ln3_b"), gate[:, GX1:GX1 + 1], None, ALU.mult)
                dve.wait_ge(set_up, 1)
                nc.vector.tensor_scalar(sb2_g[:], sb2_sum[:], gate[:, GF1:GF1 + 1], None, ALU.mult).then_inc(set_up, 1)
                dve.wait_ge(set_up, 2)

            @block.gpsimd
            def _(pool):
                pool.wait_ge(small_loaded, 8 * 16)
                for l in range(LAYERS):
                    for k, (name, swap) in enumerate((("qs", "qs_swap"), ("ks", "ks_swap"))):
                        for tab, rot, scale in ((tab_a, rot_a, name), (tab_b, rot_b, swap)):
                            last = nc.gpsimd.tensor_tensor(
                                tab[:, l, :, k, :], rot[:, :, k, :],
                                row(scale, l, DH).unsqueeze(1).to_broadcast([P, TILES, DH]), ALU.mult)
                last.then_inc(pool_setup, 1)
                pool.wait_ge(pool_setup, 1)

        loop_sems = range(min(loop_sem_numbers), max(loop_sem_numbers) + 1)

        def one_pass(i_pass, block):
            act_item, dve_item = {}, {}
            STEPS = [(t, u) for t in range(TILES) for u in SLOTS]

            @block.tensor
            def _(pe):
                def act_bank(name):
                    n = len(act_item)
                    act_item[name] = n
                    if n >= ACT_BANKS:
                        pe.wait_ge(act_emptied, n - ACT_BANKS + 1)
                    return act_psum[n % ACT_BANKS]

                def dve_bank(name):
                    n = len(dve_item)
                    dve_item[name] = n
                    if n >= DVE_BANKS:
                        pe.wait_ge(dve_emptied, n - DVE_BANKS + 1)
                    return dve_psum[n % DVE_BANKS]

                def transpose_tiles(name, src, u):
                    bank = act_bank(name)
                    for t in range(TILES):
                        last = nc.tensor.transpose(bank[:, t * P:(t + 1) * P], src[u][:, t, :], ident[:])
                    last.then_inc(act_filled, 1)

                def transpose_norm(name, ln, u):
                    pe.wait_ge(ln_done[u], ln + 1)
                    transpose_tiles(name, nrm, u)

                pe.wait_ge(w_loaded["first"], 3 * 16)
                for u in SLOTS:
                    pe.wait_ge(ctx_loaded[u], 16)
                    bank = act_bank(("ctxT", u))
                    for j in range(2):
                        last = nc.tensor.transpose(bank[:, j * CH:(j + 1) * CH], ctx_t[u][:, j, :], ident[0:CH, 0:CH])
                    last.then_inc(act_filled, 1)
                for u in SLOTS:
                    pe.wait_ge(act_emptied, act_item["ctxT", u] + 1)
                    bank = act_bank(("k", u))
                    nc.tensor.matmul(bank[:, 0:CTX], wk[:], ctxT[u][:], start=True, stop=True).then_inc(act_filled, 1)
                    bank = dve_bank(("v", u))
                    for j in range(2):
                        last = nc.tensor.matmul(bank[0:CH, j * D:(j + 1) * D], ctxT[u][:, j * CH:(j + 1) * CH], wv[:],
                                                start=True, stop=True)
                    last.then_inc(dve_filled, 1)
                for u in SLOTS:
                    transpose_norm(("hT_first", u), LN_XATTN, u)
                for u in SLOTS:
                    pe.wait_ge(act_emptied, act_item["hT_first", u] + 1)
                    bank = act_bank(("q", u))
                    nc.tensor.matmul(bank[:], wq[:], hT[u][:], start=True, stop=True).then_inc(act_filled, 1)
                for u in SLOTS:
                    pe.wait_ge(act_emptied, act_item["q", u] + 1)
                    for t in range(TILES):
                        bank = dve_bank(("s_first", u, t))
                        nc.tensor.matmul(bank[:, 0:CTX], qT[u][:, 0, t * P:(t + 1) * P], kcT[u][:, 0, :],
                                         start=True, stop=True).then_inc(dve_filled, 1)
                for u in SLOTS:
                    pe.wait_ge(exp_done[u], SM_FIRST + 1)
                    for j, bank in ((0, dve_bank(("pt_first", u))), (1, act_bank(("pt_first", u)))):
                        for t in range(TILES):
                            last = nc.tensor.transpose(bank[0:CH, t * P:(t + 1) * P],
                                                       prob[u][:, t, j * CH:(j + 1) * CH], ident[:])
                        last.then_inc(dve_filled if j == 0 else act_filled, 1)
                for u in SLOTS:
                    pe.wait_ge(dve_emptied, dve_item["pt_first", u] + 1)
                    pe.wait_ge(act_emptied, act_item["pt_first", u] + 1)
                    bank = dve_bank(("o_first", u))
                    for t in range(TILES):
                        for j, pt in enumerate((pta, ptb)):
                            last = nc.tensor.matmul(bank[:, t * D:(t + 1) * D], pt[u][0:CH, t, :], v_ctx[u][:, j, :],
                                                    start=(j == 0), stop=(j == 1))
                    last.then_inc(dve_filled, 1)

                pe.wait_ge(w_loaded["local"], 6 * 16)
                for l in range(LAYERS):
                    for u in SLOTS:
                        if l == 0:
                            pe.wait_ge(ln_done[u], LN_OUTER + 1)
                        else:
                            pe.wait_ge(dve_emptied, dve_item["ff_out", l - 1, u] + 1)
                        transpose_tiles(("hTs", l, u), y, u)
                    attn_w = wqkv[:, l, :]

                    def project(t, u):
                        if t == 0:
                            pe.wait_ge(act_emptied, act_item["hTs", l, u] + 1)
                        h = hTs[u][:, WINDOW + t * P:WINDOW + (t + 1) * P]
                        for k in range(2):
                            bank = act_bank(("qk", l, t, u, k))
                            nc.tensor.matmul(bank[:], h, attn_w[:, k * INNER:(k + 1) * INNER], start=True, stop=True)\
                              .then_inc(act_filled, 1)
                        for j in ([t] if t < TILES - 1 else [t, t + 1]):
                            n = P if j < TILES else WINDOW
                            bank = act_bank(("v_loc", l, j, u))
                            nc.tensor.matmul(bank[0:n, :], hTs[u][:, j * P:j * P + n], attn_w[:, 2 * INNER:3 * INNER],
                                             start=True, stop=True).then_inc(act_filled, 1)

                    def turn(t, u):
                        pe.wait_ge(turned_ready[u], TILES * l + t + 1)
                        bank = act_bank(("qT", l, t, u))
                        for c in range(INNER // P):
                            last = nc.tensor.transpose(bank[:, c * P:(c + 1) * P], turned[u][:, 0, c * P:(c + 1) * P], ident[:])
                        last.then_inc(act_filled, 1)
                        pe.wait_ge(k_ready[u], TILES * l + t + 1)
                        bank = dve_bank(("kT", l, t, u))
                        for c in range(INNER // P):
                            last = nc.tensor.transpose(bank[:, c * P:(c + 1) * P], turned[u][:, 1, c * P:(c + 1) * P], ident[:])
                        last.then_inc(dve_filled, 1)

                    for n in range(len(STEPS) + 2):
                        if n < len(STEPS):
                            project(*STEPS[n])
                        if n >= 2:
                            turn(*STEPS[n - 2])

                    def scores(t, u):
                        if t == 0:
                            pe.wait_ge(act_emptied, act_item["qT", l, TILES - 1, u] + 1)
                            pe.wait_ge(dve_emptied, dve_item["kT", l, TILES - 1, u] + 1)
                        for g in range(2):
                            for odd in range(2):
                                bank = dve_bank(("s_local", l, t, u, g, odd))
                                for i in range(2):
                                    c = 2 * g + i
                                    half = slice(DH * odd, DH * odd + DH)
                                    last = nc.tensor.matmul(bank[:, i * KEYS:(i + 1) * KEYS], qT[u][half, c, t * P:(t + 1) * P],
                                                            kT[u][half, c, t * P:t * P + KEYS], start=True, stop=True)
                                last.then_inc(dve_filled, 1)

                    def turn_probs(t, u):
                        pe.wait_ge(exp_done[u], sm_local(l, t) + 1)
                        for g in range(2):
                            bank = dve_bank(("pta", l, t, u, g))
                            for i in range(4):
                                last = nc.tensor.transpose(bank[:, i * P:(i + 1) * P], prob[u][:, 4 * g + i, 0:P], ident[:])
                            last.then_inc(dve_filled, 1)
                            bank = act_bank(("ptb", l, t, u, g))
                            for i in range(4):
                                last = nc.tensor.transpose(bank[0:WINDOW, i * P:(i + 1) * P], prob[u][:, 4 * g + i, P:KEYS], ident[:])
                            last.then_inc(act_filled, 1)

                    def mix_values(t, u):
                        pe.wait_ge(dve_emptied, dve_item["pta", l, t, u, 1] + 1)
                        pe.wait_ge(act_emptied, act_item["ptb", l, t, u, 1] + 1)
                        bank = dve_bank(("o_local", l, t, u))
                        for h in range(HEADS):
                            dst = bank[:, h * DH:(h + 1) * DH]
                            nc.tensor.matmul(dst, pta[u][:, h, :], v_loc[u][:, t, h * DH:(h + 1) * DH], start=True, stop=False)
                            last = nc.tensor.matmul(dst, ptb[u][0:WINDOW, h, :], v_loc[u][0:WINDOW, t + 1, h * DH:(h + 1) * DH],
                                                    start=False, stop=True)
                        last.then_inc(dve_filled, 1)

                    def turn_out(t, u):
                        pe.wait_ge(dve_emptied, dve_item["o_local", l, t, u] + 1)
                        bank = act_bank(("oT", l, t, u))
                        for c in range(INNER // P):
                            last = nc.tensor.transpose(bank[:, c * P:(c + 1) * P], otok[u][:, c * P:(c + 1) * P], ident[:])
                        last.then_inc(act_filled, 1)

                    def project_out(t, u):
                        pe.wait_ge(act_emptied, act_item["oT", l, t, u] + 1)
                        bank = dve_bank(("attn_out", l, t, u))
                        for c in range(INNER // P):
                            last = nc.tensor.matmul(bank[:, 0:D], oT[u][:, c, :], wo[:, l, c, :],
                                                    start=(c == 0), stop=(c == INNER // P - 1))
                        last.then_inc(dve_filled, 1)

                    for n in range(len(STEPS) + 4):
                        for lag, stage in ((0, scores), (2, mix_values), (3, turn_out), (4, project_out), (1, turn_probs)):
                            if 0 <= n - lag < len(STEPS):
                                stage(*STEPS[n - lag])

                    for u in SLOTS:
                        transpose_norm(("hT_ff", l, u), LN_FF[l], u)
                    for m, w in enumerate(HID_W):
                        for u in SLOTS:
                            if m == 0:
                                pe.wait_ge(act_emptied, act_item["hT_ff", l, u] + 1)
                            bank = act_bank(("ff_g", l, m, u))
                            nc.tensor.matmul(bank[0:w, :], w1[:, l, HID + m * P:HID + m * P + w], hT[u][:],
                                             start=True, stop=True).then_inc(act_filled, 1)
                            bank = dve_bank(("ff_a", l, m, u))
                            nc.tensor.matmul(bank[0:w, :], w1[:, l, m * P:m * P + w], hT[u][:],
                                             start=True, stop=True).then_inc(dve_filled, 1)
                    for u in SLOTS:
                        pe.wait_ge(dve_emptied, dve_item["ff_a", l, len(HID_W) - 1, u] + 1)
                        bank = dve_bank(("ff_out", l, u))
                        for t in range(TILES):
                            for m, w in enumerate(HID_W):
                                last = nc.tensor.matmul(bank[:, t * D:(t + 1) * D], qT[u][0:w, m, t * P:(t + 1) * P],
                                                        w2[0:w, l, m, :], start=(m == 0), stop=(m == len(HID_W) - 1))
                        last.then_inc(dve_filled, 1)

                pe.wait_ge(w_loaded["cross"], 8 * 16)
                for u in SLOTS:
                    bank = act_bank(("kc", u))
                    for c in range(2):
                        last = nc.tensor.matmul(bank[:, c * CTX:(c + 1) * CTX], w_cak[:, c, :], ctxT[u][:], start=True, stop=True)
                    last.then_inc(act_filled, 1)
                    bank = dve_bank(("vc", u))
                    for j in range(2):
                        last = nc.tensor.matmul(bank[0:CH, j * D:(j + 1) * D], ctxT[u][:, j * CH:(j + 1) * CH], w_cav[:],
                                                start=True, stop=True)
                    last.then_inc(dve_filled, 1)
                for u in SLOTS:
                    pe.wait_ge(ln_done[u], LN_TGT + 1)
                    transpose_tiles(("hT_sa", u), y, u)
                for u in SLOTS:
                    pe.wait_ge(act_emptied, act_item["hT_sa", u] + 1)
                    bank = act_bank(("v_sa", u))
                    nc.tensor.matmul(bank[:], w_sa[:, 2 * D:3 * D], hT[u][:], start=True, stop=True).then_inc(act_filled, 1)
                    for j in range(2):
                        bank = act_bank(("qk_sa", u, j))
                        for i in range(2):
                            t = 2 * j + i
                            dst = bank[:, 2 * D * i:2 * D * (i + 1)]
                            nc.tensor.matmul(dst, hT[u][:, t * P:(t + 1) * P], w_sa[:, 0:2 * D], start=True, stop=False)
                            last = nc.tensor.matmul(dst, ones_row[:], row("bqk_sa", 0, 2 * D, 1), start=False, stop=True)
                        last.then_inc(act_filled, 1)
                for u in SLOTS:
                    pe.wait_ge(act_emptied, act_item["v_sa", u] + 1)
                    bank = dve_bank(("sa_out", u))
                    for t in range(TILES):
                        last = nc.tensor.matmul(bank[:, t * D:(t + 1) * D], qT[u][:, 0, t * P:(t + 1) * P], w_sao[:],
                                                start=True, stop=True)
                    last.then_inc(dve_filled, 1)
                for u in SLOTS:
                    transpose_norm(("hT_ca", u), LN_1, u)
                for u in SLOTS:
                    pe.wait_ge(act_emptied, act_item["hT_ca", u] + 1)
                    for c in range(2):
                        bank = act_bank(("q_ca", u, c))
                        nc.tensor.matmul(bank[:], w_caq[:, c, :], hT[u][:], start=True, stop=True).then_inc(act_filled, 1)

                def ca_scores(t, u):
                    if t == 0:
                        pe.wait_ge(act_emptied, act_item["q_ca", u, 1] + 1)
                    for j in range(4):
                        bank = dve_bank(("s_ca", t, u, j))
                        for c in range(2):
                            part = slice(32 * j, 32 * j + 32)
                            last = nc.tensor.matmul(bank[:, c * CTX:(c + 1) * CTX], qT[u][part, c, t * P:(t + 1) * P],
                                                    kcT[u][part, c, :], start=True, stop=True)
                        last.then_inc(dve_filled, 1)

                def ca_turn_probs(t, u):
                    pe.wait_ge(exp_done[u], sm_cross(t) + 1)
                    for g in range(2):
                        for j, bank, filled in ((0, dve_bank(("pta_ca", t, u, g)), dve_filled),
                                                (1, act_bank(("ptb_ca", t, u, g)), act_filled)):
                            for i in range(4):
                                last = nc.tensor.transpose(bank[0:CH, i * P:(i + 1) * P],
                                                           prob[u][:, 4 * g + i, j * CH:(j + 1) * CH], ident[:])
                            last.then_inc(filled, 1)

                def ca_mix(t, u):
                    pe.wait_ge(dve_emptied, dve_item["pta_ca", t, u, 1] + 1)
                    pe.wait_ge(act_emptied, act_item["ptb_ca", t, u, 1] + 1)
                    bank = dve_bank(("o_ca", t, u))
                    for h in range(CA_HEADS):
                        f = slice(h * CA_DH, (h + 1) * CA_DH)
                        for j, pt in enumerate((pta, ptb)):
                            last = nc.tensor.matmul(bank[:, f], pt[u][0:CH, h, :], v_ctx[u][:, j, f],
                                                    start=(j == 0), stop=(j == 1))
                    last.then_inc(dve_filled, 1)

                def ca_turn_out(t, u):
                    pe.wait_ge(dve_emptied, dve_item["o_ca", t, u] + 1)
                    bank = act_bank(("oT_ca", t, u))
                    nc.tensor.transpose(bank[:, 0:P], otok[u][:, 0:P], ident[:]).then_inc(act_filled, 1)

                def ca_project_out(t, u):
                    pe.wait_ge(act_emptied, act_item["oT_ca", t, u] + 1)
                    bank = dve_bank(("ca_out", t, u))
                    nc.tensor.matmul(bank[:, 0:D], oT[u][:, 0, :], w_cao[:], start=True, stop=True).then_inc(dve_filled, 1)

                for n in range(len(STEPS) + 4):
                    for lag, stage in ((0, ca_scores), (2, ca_mix), (3, ca_turn_out), (4, ca_project_out), (1, ca_turn_probs)):
                        if 0 <= n - lag < len(STEPS):
                            stage(*STEPS[n - lag])

                for u in SLOTS:
                    transpose_norm(("hT_lin", u), LN_2, u)
                for m in range(FF // P):
                    for u in SLOTS:
                        if m == 0:
                            pe.wait_ge(act_emptied, act_item["hT_lin", u] + 1)
                        bank = act_bank(("lin1", m, u))
                        nc.tensor.matmul(bank[:], w_l1[:, m * P:(m + 1) * P], hT[u][:], start=True, stop=True)\
                          .then_inc(act_filled, 1)
                for u in SLOTS:
                    pe.wait_ge(act_emptied, act_item["lin1", FF // P - 1, u] + 1)
                    bank = dve_bank(("lin2", u))
                    for t in range(TILES):
                        for m in range(FF // P):
                            last = nc.tensor.matmul(bank[:, t * D:(t + 1) * D], qT[u][:, m, t * P:(t + 1) * P], w_l2[:, m, :],
                                                    start=(m == 0), stop=(m == FF // P - 1))
                    last.then_inc(dve_filled, 1)

                pe.wait_ge(w_loaded["moe"], 6 * 16)
                for u in SLOTS:
                    transpose_norm(("hT_moe", u), LN_MOE, u)
                for u in SLOTS:
                    pe.wait_ge(act_emptied, act_item["hT_moe", u] + 1)
                    bank = dve_bank(("logits", u))
                    for t in range(TILES):
                        last = nc.tensor.matmul(bank[:, t * EXPERTS:(t + 1) * EXPERTS], hT[u][:, t * P:(t + 1) * P], w_rt[:],
                                                start=True, stop=True)
                    last.then_inc(dve_filled, 1)
                for u in SLOTS:
                    pe.wait_ge(cw_ready[u], 1)
                    bank = act_bank(("cwT", u))
                    for t in range(TILES):
                        last = nc.tensor.transpose(bank[0:EXPERTS, t * P:(t + 1) * P], cw[u][:, t, :], ident[:])
                    last.then_inc(act_filled, 1)
                    bank = dve_bank(("cwT_hm", u))[:, 0:SEQ // 2].bitcast(BF16)
                    for t in range(TILES):
                        last = nc.tensor.transpose(bank[:, t * P:(t + 1) * P], cw_hm[u][:, t, :], identb[:])
                    last.then_inc(dve_filled, 1)
                    bank = dve_bank(("cwT_lo", u))[:, 0:SEQ // 2].bitcast(BF16)
                    for t in range(TILES):
                        last = nc.tensor.transpose(bank[0:EXPERTS, t * P:(t + 1) * P], cw_lo[u][:, t, :], identb[:])
                    last.then_inc(dve_filled, 1)

                def expert_hidden(u, c):
                    bank = act_bank(("moe_h", u, c))
                    w = w_m1[:, c * P:(c + 1) * P] if c < ROUTED else w_s1[:, c - ROUTED, :]
                    nc.tensor.matmul(bank[:], w, hT[u][:], start=True, stop=True).then_inc(act_filled, 1)
                    if c < ROUTED:
                        if c == 0:
                            pe.wait_ge(dve_emptied, dve_item["cwT_lo", u] + 1)
                        bank = dve_bank(("moe_w", u, c))
                        nc.tensor.matmul(bank[:], sel[:, c, :], cwT_hm[u], start=True, stop=False)
                        nc.tensor.matmul(bank[:], sel[0:EXPERTS, c, :], cwT_lo[u], start=False, stop=True)\
                          .then_inc(dve_filled, 1)

                def expert_out(u, c):
                    if c < ROUTED:
                        pe.wait_ge(dve_emptied, dve_item["moe_w", u, c] + 1)
                    else:
                        pe.wait_ge(act_emptied, act_item["moe_h", u, c] + 1)
                    if c == 0 and u > 0:
                        pe.wait_ge(moe_emptied, u)
                    w = w_m2[:, c, :] if c < ROUTED else w_s2[:, c - ROUTED, :]
                    nc.tensor.matmul(moe_psum[:], w, weighed[u][:, c % 3, :], start=(c == 0), stop=False)

                for u in SLOTS:
                    for c in range(ROUTED + SHARED + 2):
                        if c < ROUTED + SHARED:
                            expert_hidden(u, c)
                        if c >= 2:
                            expert_out(u, c - 2)
                        if c == ROUTED and u > 0:
                            pe.wait_ge(moe_emptied, u)
                            bank = dve_bank(("moe_out", u - 1))
                            for t in range(TILES):
                                last = nc.tensor.transpose(bank[:, t * P:(t + 1) * P], qT[u - 1][:, 0, t * P:(t + 1) * P], ident[:])
                            last.then_inc(dve_filled, 1)
                    pe.wait_ge(act_emptied, act_item["cwT", u] + 1)
                    nc.tensor.matmul(moe_psum[:], b_m2[:], cwT[u], start=False, stop=True).then_inc(moe_filled, 1)
                u = SLOTS[-1]
                pe.wait_ge(moe_emptied, u + 1)
                bank = dve_bank(("moe_out", u))
                for t in range(TILES):
                    last = nc.tensor.transpose(bank[:, t * P:(t + 1) * P], qT[u][:, 0, t * P:(t + 1) * P], ident[:])
                last.then_inc(dve_filled, 1)

            @block.scalar
            def _(act):
                taken = [0]

                def filled(name):
                    n = act_item[name]
                    assert n == taken[0], name
                    taken[0] += 1
                    act.wait_ge(act_filled, n + 1)
                    return act_psum[n % ACT_BANKS]

                def copy_bank(name, dst, bias=None, scale=1.0, n=P, w=SEQ):
                    bank = filled(name)
                    if bias is None:
                        nc.scalar.copy(dst, bank[0:n, 0:w]).then_inc(act_emptied, 1)
                    else:
                        nc.scalar.activation(dst, bank[0:n, 0:w], ACT.Identity, bias=bias, scale=scale).then_inc(act_emptied, 1)

                def exponentials(u, number, tiles, width, scale_of):
                    act.wait_ge(peak_ready[u], number + 1)
                    for i in range(tiles):
                        last = nc.scalar.activation(prob[u][:, i, 0:width], prob[u][:, i, 0:width], ACT.Exp,
                                                    bias=nbias[u][:, i:i + 1], scale=scale_of(i), accum_out=sums[u][:, i:i + 1])
                    last.then_inc(exp_done[u], 1)

                for u in SLOTS:
                    copy_bank(("ctxT", u), ctxT[u][:], w=CTX)
                for u in SLOTS:
                    copy_bank(("k", u), kcT[u][:, 0, :], bias=col("bk"), w=CTX)
                for u in SLOTS:
                    copy_bank(("hT_first", u), hT[u][:])
                for u in SLOTS:
                    copy_bank(("q", u), qT[u][:, 0, :], bias=col("bq"))
                for u in SLOTS:
                    exponentials(u, SM_FIRST, TILES, CTX, lambda i: D ** -0.5)
                for u in SLOTS:
                    copy_bank(("pt_first", u), ptb[u][0:CH, 0:TILES, :].rearrange("p t q -> p (t q)"), n=CH)

                for l in range(LAYERS):
                    for u in SLOTS:
                        bank = filled(("hTs", l, u))
                        nc.scalar.copy(hTs[u][0:D // 2, WINDOW:], bank[0:D // 2, :])
                        nc.scalar.copy(hTs[u][D // 2:D, WINDOW + 1:], bank[D // 2:D, 0:SEQ - 1]).then_inc(act_emptied, 1)

                    def take_projection(t, u):
                        if t > 0:
                            act.wait_ge(turned_ready[u], TILES * l + t)
                        for k in range(2):
                            copy_bank(("qk", l, t, u, k), raw[u][:, k, :])
                        act.wait_ge(act_emptied, act_item["qk", l, t, u, 1] + 1)
                        nc.scalar.activation(partner[u], raw[u], ACT.Square).then_inc(sq_ready[u], 1)
                        for j in ([t] if t < TILES - 1 else [t, t + 1]):
                            n = P if j < TILES else WINDOW
                            copy_bank(("v_loc", l, j, u), v_loc[u][0:n, j, :], n=n)

                    def take_turned(t, u):
                        bank = filled(("qT", l, t, u))
                        nc.scalar.copy(qT[u][:, :, t * P:(t + 1) * P], bank[:].rearrange("p (c q) -> p c q", q=P))\
                          .then_inc(act_emptied, 1)

                    for n in range(len(STEPS) + 2):
                        if n < len(STEPS):
                            take_projection(*STEPS[n])
                        if n >= 2:
                            take_turned(*STEPS[n - 2])

                    def exp_local(t, u):
                        exponentials(u, sm_local(l, t), HEADS, KEYS, lambda i: rnorm[u][:, t, i:i + 1])

                    def take_ptb(t, u):
                        for g in range(2):
                            copy_bank(("ptb", l, t, u, g), ptb[u][0:WINDOW, 4 * g:4 * g + 4, :].rearrange("p t q -> p (t q)"), n=WINDOW)

                    def take_out(t, u):
                        copy_bank(("oT", l, t, u), hT[u][:])

                    for n in range(len(STEPS) + 4):
                        for lag, stage in ((3, take_out), (1, take_ptb), (0, exp_local)):
                            if 0 <= n - lag < len(STEPS):
                                stage(*STEPS[n - lag])

                    for u in SLOTS:
                        copy_bank(("hT_ff", l, u), hT[u][:], bias=col("ln_b", l), scale=col("ln_g", l))
                    for m, w in enumerate(HID_W):
                        for u in SLOTS:
                            bank = filled(("ff_g", l, m, u))
                            nc.scalar.activation(gel[u][0:w, m, :], bank[0:w, :], ACT.Gelu, bias=col("b1g", 3 * l + m, w))\
                              .then_inc(act_emptied, 1)

                for u in SLOTS:
                    bank = filled(("kc", u))
                    for c in range(2):
                        last = nc.scalar.activation(kcT[u][:, c, :], bank[:, c * CTX:(c + 1) * CTX], ACT.Identity,
                                                    bias=col("bk_ca", c))
                    last.then_inc(act_emptied, 1)
                for u in SLOTS:
                    copy_bank(("hT_sa", u), hT[u][:])
                for u in SLOTS:
                    copy_bank(("v_sa", u), qT[u][:, 0, :], bias=col("bv_sa"))
                    for j in range(2):
                        copy_bank(("qk_sa", u, j), raw[u][:, j, :])
                for u in SLOTS:
                    act.wait_ge(diag_ready[u], 1)
                    nc.scalar.activation(diag[u][:, 2, :], diag[u][:, 1, :], ACT.Exp, scale=float(D) ** 0.5)\
                      .then_inc(diag_exp[u], 1)
                for u in SLOTS:
                    copy_bank(("hT_ca", u), hT[u][:], bias=col("ln1_b"), scale=col("ln1_g"))
                for u in SLOTS:
                    for c in range(2):
                        copy_bank(("q_ca", u, c), qT[u][:, c, :], bias=col("bq_ca", c))

                def ca_exp(t, u):
                    exponentials(u, sm_cross(t), CA_HEADS, CTX, lambda i: CA_DH ** -0.5)

                def ca_take_ptb(t, u):
                    for g in range(2):
                        copy_bank(("ptb_ca", t, u, g), ptb[u][0:CH, 4 * g:4 * g + 4, :].rearrange("p t q -> p (t q)"), n=CH)

                def ca_take_out(t, u):
                    copy_bank(("oT_ca", t, u), oT[u][:, 0, :], w=P)

                for n in range(len(STEPS) + 4):
                    for lag, stage in ((3, ca_take_out), (1, ca_take_ptb), (0, ca_exp)):
                        if 0 <= n - lag < len(STEPS):
                            stage(*STEPS[n - lag])

                for u in SLOTS:
                    copy_bank(("hT_lin", u), hT[u][:], bias=col("ln2_b"), scale=col("ln2_g"))
                for m in range(FF // P):
                    for u in SLOTS:
                        bank = filled(("lin1", m, u))
                        nc.scalar.activation(qT[u][:, m, :], bank[:], ACT.Relu, bias=col("lin1_b", m)).then_inc(act_emptied, 1)

                for u in SLOTS:
                    copy_bank(("hT_moe", u), hT[u][:])
                for u in SLOTS:
                    act.wait_ge(logit_ready[u], 1)
                    nc.scalar.activation(expw[u], logit[u], ACT.Exp).then_inc(expw_ready[u], 1)
                for u in SLOTS:
                    copy_bank(("cwT", u), cwT[u], n=EXPERTS)
                for u in SLOTS:
                    for c in range(ROUTED + SHARED):
                        bank = filled(("moe_h", u, c))
                        if c < ROUTED:
                            if c >= 3:
                                act.wait_ge(dve_emptied, dve_item["moe_w", u, c - 3] + 1)
                            dst, bias = hid[u][:, c % 3, :], col("moe_b1", c)
                        else:
                            dst, bias = weighed[u][:, c % 3, :], col("sb1", c - ROUTED)
                        nc.scalar.activation(dst, bank[:], ACT.Silu, bias=bias).then_inc(act_emptied, 1)
                    act.wait_ge(moe_filled, u + 1)
                    nc.scalar.activation(qT[u][:, 0, :], moe_psum[:], ACT.Identity, bias=sb2_g[:], scale=gate[:, GF1:GF1 + 1])\
                      .then_inc(moe_emptied, 1)
                assert taken[0] == len(act_item)

            @block.vector
            def _(dve):
                taken = [0]
                links = [0]

                def filled(name):
                    n = dve_item[name]
                    assert n == taken[0], name
                    taken[0] += 1
                    dve.wait_ge(dve_filled, n + 1)
                    return dve_psum[n % DVE_BANKS]

                def link(ins):
                    links[0] += 1
                    ins.then_inc(dve_chain, 1)
                    dve.wait_ge(dve_chain, links[0])

                def norm_stats(src, u):
                    for t in range(TILES):
                        last = nc.vector.bn_stats(stats[u][:, t, :], src[u][:, t, :])
                    link(last)
                    for t in range(TILES):
                        last = nc.vector.bn_aggr(mv[u][:, t, :], stats[u][:, t, :])
                    last.then_inc(ln_stats[u], 1)

                def norm_apply(ln, src, dst, u):
                    dve.wait_ge(ln_rstd[u], ln + 1)
                    for t in range(TILES):
                        last = nc.vector.tensor_scalar(dst[u][:, t, :], src[u][:, t, :], mv[u][:, t, 0:1], rstd[u][:, t:t + 1],
                                                       ALU.subtract, ALU.mult)
                    last.then_inc(ln_done[u], 1)

                def norm(ln, src, dst, before=None):
                    for u in SLOTS:
                        if before is not None:
                            before(u)
                        norm_stats(src, u)
                    for u in SLOTS:
                        norm_apply(ln, src, dst, u)

                def mask_and_peak(bank, at, width, mask, u, i):
                    return nc.vector.tensor_tensor_reduce(out=prob[u][:, i, 0:width], in0=bank[:, at:at + width], in1=mask,
                                                          scale=1.0, scalar=LOWEST, op0=ALU.add, op1=ALU.max,
                                                          accum_out=peak[u][:, i:i + 1])

                def reciprocal_sums(u, number, n):
                    dve.wait_ge(exp_done[u], number + 1)
                    nc.vector.reciprocal(rinv[u][:, 0:n], sums[u][:, 0:n]).then_inc(rinv_ready[u], 1)

                for u in SLOTS:
                    bank = filled(("v", u))
                    nc.vector.tensor_tensor(v_ctx[u][:], bank[0:CH, 0:2 * D].rearrange("p (j n) -> p j n", j=2),
                                            row("bv", n=CH).unsqueeze(1).to_broadcast([CH, 2, D]), ALU.add)\
                      .then_inc(dve_emptied, 1)
                norm(LN_XATTN, x, nrm, before=lambda u: dve.wait_ge(x_loaded[u], 16))
                for u in SLOTS:
                    for t in range(TILES):
                        bank = filled(("s_first", u, t))
                        mask_and_peak(bank, 0, CTX, no_mask[:], u, t).then_inc(dve_emptied, 1)
                    dve.wait_ge(dve_emptied, dve_item["s_first", u, TILES - 1] + 1)
                    nc.vector.tensor_scalar(nbias[u][:, 0:TILES], peak[u][:, 0:TILES], -D ** -0.5, None, ALU.mult)\
                      .then_inc(peak_ready[u], 1)
                for u in SLOTS:
                    bank = filled(("pt_first", u))
                    nc.vector.tensor_copy(pta[u][0:CH, 0:TILES, :].rearrange("p t q -> p (t q)"), bank[0:CH, :])\
                      .then_inc(dve_emptied, 1)
                for u in SLOTS:
                    reciprocal_sums(u, SM_FIRST, TILES)
                    dve.wait_ge(rinv_ready[u], SM_FIRST + 1)
                    link(nc.vector.tensor_scalar(rinv[u][:, 0:TILES], rinv[u][:, 0:TILES], gate[:, GX0:GX0 + 1], None, ALU.mult))
                    bank = filled(("o_first", u))
                    for t in range(TILES):
                        last = nc.vector.scalar_tensor_tensor(out=x[u][:, t, :], in0=bank[:, t * D:(t + 1) * D],
                                                              scalar=rinv[u][:, t:t + 1], in1=x[u][:, t, :],
                                                              op0=ALU.mult, op1=ALU.add)
                    last.then_inc(dve_emptied, 1)
                norm(LN_OUTER, x, y, before=lambda u: dve.wait_ge(dve_emptied, dve_item["o_first", u] + 1))

                for l in range(LAYERS):
                    def sum_squares(t, u):
                        dve.wait_ge(sq_ready[u], TILES * l + t + 1)
                        nc.vector.tensor_reduce(sumsq[u][:, t, :], partner[u].rearrange("p a (h d) -> p (a h) d", d=DH),
                                                AX.X, ALU.add).then_inc(sumsq_ready[u], 1)

                    def rotate_own(t, u):
                        heads = "p a (h d) -> p a h d"
                        nc.vector.tensor_tensor(turned[u].rearrange(heads, d=DH), raw[u].rearrange(heads, d=DH),
                                                tab_a[:, l, t, :, :].unsqueeze(2).to_broadcast([P, 2, HEADS, DH]), ALU.mult)\
                          .then_inc(own_ready[u], 1)

                    def add_partner(t, u):
                        dve.wait_ge(own_ready[u], TILES * l + t + 1)
                        dve.wait_ge(partner_ready[u], TILES * l + t + 1)
                        nc.vector.tensor_tensor(turned[u], turned[u], partner[u], ALU.add).then_inc(turned_ready[u], 1)

                    def take_k(t, u):
                        bank = filled(("kT", l, t, u))
                        nc.vector.tensor_copy(kT[u][:, :, WINDOW + t * P:WINDOW + (t + 1) * P],
                                              bank[:].rearrange("p (c q) -> p c q", q=P)).then_inc(dve_emptied, 1)

                    for n in range(len(STEPS) + 2):
                        if n >= 2:
                            take_k(*STEPS[n - 2])
                        if n < len(STEPS):
                            sum_squares(*STEPS[n])
                            rotate_own(*STEPS[n])
                        if 1 <= n <= len(STEPS):
                            add_partner(*STEPS[n - 1])

                    def take_scores(t, u):
                        mask = masks[:, 0 if t == 0 else 1, :]
                        for g in range(2):
                            for odd in range(2):
                                bank = filled(("s_local", l, t, u, g, odd))
                                for i in range(2):
                                    last = mask_and_peak(bank, i * KEYS, KEYS, mask, u, 2 * (2 * g + i) + odd)
                                last.then_inc(dve_emptied, 1)
                        dve.wait_ge(dve_emptied, dve_item["s_local", l, t, u, 1, 1] + 1)
                        if t == 0:
                            dve.wait_ge(rnorm_ready[u], TILES * (l + 1))
                        nc.vector.scalar_tensor_tensor(out=nbias[u][:], in0=peak[u][:], scalar=-1.0, in1=rnorm[u][:, t, 0:HEADS],
                                                       op0=ALU.mult, op1=ALU.mult).then_inc(peak_ready[u], 1)

                    def take_pta(t, u):
                        reciprocal_sums(u, sm_local(l, t), HEADS)
                        for g in range(2):
                            bank = filled(("pta", l, t, u, g))
                            nc.vector.tensor_copy(pta[u][:, 4 * g:4 * g + 4, :].rearrange("p t q -> p (t q)"), bank[:])\
                              .then_inc(dve_emptied, 1)

                    def divide(t, u):
                        dve.wait_ge(rinv_ready[u], sm_local(l, t) + 1)
                        bank = filled(("o_local", l, t, u))
                        nc.vector.tensor_tensor(otok[u].rearrange("p (h d) -> p h d", d=DH),
                                                bank[:].rearrange("p (h d) -> p h d", d=DH),
                                                rinv[u][:].unsqueeze(2).to_broadcast([P, HEADS, DH]), ALU.mult)\
                          .then_inc(dve_emptied, 1)

                    def add_attention(t, u):
                        bank = filled(("attn_out", l, t, u))
                        nc.vector.tensor_tensor(y[u][:, t, :], bank[:, 0:D], y[u][:, t, :], ALU.add).then_inc(dve_emptied, 1)

                    for n in range(len(STEPS) + 4):
                        for lag, stage in ((0, take_scores), (2, divide), (4, add_attention), (1, take_pta)):
                            if 0 <= n - lag < len(STEPS):
                                stage(*STEPS[n - lag])

                    norm(LN_FF[l], shifted, nrm, before=lambda u: dve.wait_ge(shift_done[u], 4 * 16 * (l + 1)))
                    for m, w in enumerate(HID_W):
                        for u in SLOTS:
                            bank = filled(("ff_a", l, m, u))
                            dve.wait_ge(act_emptied, act_item["ff_g", l, m, u] + 1)
                            nc.vector.scalar_tensor_tensor(out=qT[u][0:w, m, :], in0=bank[0:w, :], scalar=col("b1a", 3 * l + m, w),
                                                           in1=gel[u][0:w, m, :], op0=ALU.add, op1=ALU.mult)\
                              .then_inc(dve_emptied, 1)
                    for u in SLOTS:
                        bank = filled(("ff_out", l, u))
                        dve.wait_ge(res_ready[u], l + 1)
                        nc.vector.tensor_tensor(flat(y[u]), bank[:], flat(res[u]), ALU.add).then_inc(dve_emptied, 1)

                def gated(u):
                    dve.wait_ge(dve_emptied, dve_item["ff_out", LAYERS - 1, u] + 1)
                    link(nc.vector.scalar_tensor_tensor(out=flat(x[u]), in0=flat(y[u]), scalar=gate[:, GF0:GF0 + 1],
                                                        in1=flat(x[u]), op0=ALU.mult, op1=ALU.add))

                norm(LN_TGT, x, y, before=gated)
                for u in SLOTS:
                    bank = filled(("vc", u))
                    nc.vector.tensor_tensor(v_ctx[u][:], bank[0:CH, 0:2 * D].rearrange("p (j n) -> p j n", j=2),
                                            row("bv_ca", n=CH).unsqueeze(1).to_broadcast([CH, 2, D]), ALU.add)\
                      .then_inc(dve_emptied, 1)
                for u in SLOTS:
                    dve.wait_ge(act_emptied, act_item["qk_sa", u, 1] + 1)
                    for t in range(TILES):
                        at = 2 * D * (t % 2)
                        last = nc.vector.tensor_tensor_reduce(out=partner[u][:, 0, t * D:(t + 1) * D], in0=raw[u][:, t // 2, at:at + D],
                                                              in1=raw[u][:, t // 2, at + D:at + 2 * D], scale=1.0, scalar=0.0,
                                                              op0=ALU.mult, op1=ALU.add, accum_out=diag[u][:, 0, t:t + 1])
                    link(last)
                    link(nc.vector.tensor_reduce(diag[u][:, 3, :], diag[u][:, 0, :].unsqueeze(2), AX.X, ALU.max))
                    nc.vector.tensor_tensor(diag[u][:, 1, :], diag[u][:, 0, :], diag[u][:, 3, :], ALU.subtract)\
                      .then_inc(diag_ready[u], 1)
                for u in SLOTS:
                    dve.wait_ge(diag_exp[u], 1)
                    link(nc.vector.reciprocal(diag[u][:, 3, :], diag[u][:, 2, :]))
                    link(nc.vector.tensor_tensor(diag[u][:, 0, :], diag[u][:, 2, :], diag[u][:, 3, :], ALU.mult))
                    bank = filled(("sa_out", u))
                    dve.wait_ge(res_ready[u], LAYERS + 1)
                    for t in range(TILES):
                        last = nc.vector.scalar_tensor_tensor(out=y[u][:, t, :], in0=bank[:, t * D:(t + 1) * D],
                                                              scalar=diag[u][:, 0, t:t + 1], in1=res[u][:, t, :],
                                                              op0=ALU.mult, op1=ALU.add)
                    last.then_inc(dve_emptied, 1)
                norm(LN_1, y, nrm, before=lambda u: dve.wait_ge(dve_emptied, dve_item["sa_out", u] + 1))

                def ca_take_scores(t, u):
                    for j in range(4):
                        bank = filled(("s_ca", t, u, j))
                        for c in range(2):
                            last = mask_and_peak(bank, c * CTX, CTX, no_mask[:], u, 4 * c + j)
                        last.then_inc(dve_emptied, 1)
                    dve.wait_ge(dve_emptied, dve_item["s_ca", t, u, 3] + 1)
                    nc.vector.tensor_scalar(nbias[u][:], peak[u][:], -CA_DH ** -0.5, None, ALU.mult).then_inc(peak_ready[u], 1)

                def ca_take_pta(t, u):
                    reciprocal_sums(u, sm_cross(t), CA_HEADS)
                    for g in range(2):
                        bank = filled(("pta_ca", t, u, g))
                        nc.vector.tensor_copy(pta[u][0:CH, 4 * g:4 * g + 4, :].rearrange("p t q -> p (t q)"), bank[0:CH, :])\
                          .then_inc(dve_emptied, 1)

                def ca_divide(t, u):
                    dve.wait_ge(rinv_ready[u], sm_cross(t) + 1)
                    bank = filled(("o_ca", t, u))
                    nc.vector.tensor_tensor(otok[u][:, 0:P].rearrange("p (h d) -> p h d", d=CA_DH),
                                            bank[:, 0:P].rearrange("p (h d) -> p h d", d=CA_DH),
                                            rinv[u][:].unsqueeze(2).to_broadcast([P, CA_HEADS, CA_DH]), ALU.mult)\
                      .then_inc(dve_emptied, 1)

                def ca_add(t, u):
                    if t == 0:
                        dve.wait_ge(res_ready[u], LAYERS + 2)
                    bank = filled(("ca_out", t, u))
                    nc.vector.tensor_tensor(y[u][:, t, :], bank[:, 0:D], res[u][:, t, :], ALU.add).then_inc(dve_emptied, 1)

                for n in range(len(STEPS) + 4):
                    for lag, stage in ((0, ca_take_scores), (2, ca_divide), (4, ca_add), (1, ca_take_pta)):
                        if 0 <= n - lag < len(STEPS):
                            stage(*STEPS[n - lag])
                norm(LN_2, y, nrm, before=lambda u: dve.wait_ge(dve_emptied, dve_item["ca_out", TILES - 1, u] + 1))

                for u in SLOTS:
                    bank = filled(("lin2", u))
                    dve.wait_ge(res_ready[u], LAYERS + 3)
                    nc.vector.tensor_tensor(flat(y[u]), bank[:], flat(res[u]), ALU.add).then_inc(dve_emptied, 1)
                norm(LN_3, y, nrm, before=lambda u: dve.wait_ge(dve_emptied, dve_item["lin2", u] + 1))

                def add_decoder(u):
                    dve.wait_ge(res_ready[u], LAYERS + 4)
                    link(nc.vector.tensor_tensor(flat(x[u]), flat(x[u]), flat(res[u]), ALU.add))

                norm(LN_MOE, x, nrm, before=add_decoder)

                for u in SLOTS:
                    bank = filled(("logits", u))
                    nc.vector.tensor_tensor(logit[u], bank[:, 0:TILES * EXPERTS].rearrange("p (t e) -> p t e", t=TILES),
                                            row("router_b", 0, EXPERTS).unsqueeze(1).to_broadcast([P, TILES, EXPERTS]), ALU.add)\
                      .then_inc(dve_emptied, 1)
                    dve.wait_ge(dve_emptied, dve_item["logits", u] + 1)
                    link(nc.vector.tensor_reduce(rsmall[u][:, 0, :], logit[u], AX.X, ALU.max))
                    nc.vector.tensor_tensor(logit[u], logit[u], rsmall[u][:, 0, :].unsqueeze(2).to_broadcast([P, TILES, EXPERTS]),
                                            ALU.subtract).then_inc(logit_ready[u], 1)
                for u in SLOTS:
                    dve.wait_ge(expw_ready[u], 1)
                    for t in range(TILES):
                        last = nc.vector.max(top[u][:, t, :], expw[u][:, t, :])
                    link(last)
                    for t in range(TILES):
                        last = nc.vector.match_replace(rest[u][:, t, :], top[u][:, t, :], expw[u][:, t, :], 0.0)
                    link(last)
                    link(nc.vector.tensor_tensor(cw[u], expw[u], rest[u], ALU.subtract))
                    link(nc.vector.tensor_reduce(rsmall[u][:, 1, :], cw[u], AX.X, ALU.add))
                    link(nc.vector.reciprocal(rsmall[u][:, 2, :], rsmall[u][:, 1, :]))
                    link(nc.vector.tensor_tensor(cw[u], cw[u], rsmall[u][:, 2, :].unsqueeze(2).to_broadcast([P, TILES, EXPERTS]),
                                                 ALU.mult))
                    high, middle = cw_hm[u][:, :, 0:EXPERTS], cw_hm[u][:, :, EXPERTS:2 * EXPERTS]
                    link(nc.vector.tensor_copy(high, cw[u]))
                    link(nc.vector.tensor_tensor(rest[u], cw[u], high, ALU.subtract))
                    link(nc.vector.tensor_copy(middle, rest[u]))
                    nc.vector.tensor_tensor(cw_lo[u], rest[u], middle, ALU.subtract).then_inc(cw_ready[u], 1)
                for u in SLOTS:
                    bank = filled(("cwT_hm", u))
                    nc.vector.tensor_copy(cwT_hm[u], bank[:, 0:SEQ // 2].bitcast(BF16)).then_inc(dve_emptied, 1)
                    bank = filled(("cwT_lo", u))
                    nc.vector.tensor_copy(cwT_lo[u], bank[0:EXPERTS, 0:SEQ // 2].bitcast(BF16)).then_inc(dve_emptied, 1)

                def final_sum(u):
                    bank = filled(("moe_out", u))
                    nc.vector.tensor_tensor(flat(y[u]), bank[:], flat(x[u]), ALU.add).then_inc(dve_emptied, 1)

                for u in SLOTS:
                    for c in range(ROUTED):
                        bank = filled(("moe_w", u, c))
                        dve.wait_ge(act_emptied, act_item["moe_h", u, c] + 1)
                        nc.vector.tensor_tensor(weighed[u][:, c % 3, :], bank[:], hid[u][:, c % 3, :], ALU.mult)\
                          .then_inc(dve_emptied, 1)
                    if u > 0:
                        final_sum(u - 1)
                final_sum(SLOTS[-1])
                assert taken[0] == len(dve_item)

            @block.gpsimd
            def _(pool):
                links = [0]

                def link(ins):
                    links[0] += 1
                    ins.then_inc(pool_chain, 1)
                    pool.wait_ge(pool_chain, links[0])

                def norm_rstd(ln):
                    for u in SLOTS:
                        pool.wait_ge(ln_stats[u], ln + 1)
                        link(nc.gpsimd.tensor_scalar(rstd[u][:], mv[u][:, :, 1], EPS, None, ALU.add))
                        nc.gpsimd.tensor_tensor(rstd[u][:], rstd[u][:], neg_half[:, 0:TILES], ALU.pow).then_inc(ln_rstd[u], 1)

                def add_bias(u, bias):
                    nc.gpsimd.tensor_tensor(res[u][:], y[u][:], bias.unsqueeze(1).to_broadcast([P, TILES, D]), ALU.add)\
                      .then_inc(res_ready[u], 1)

                def scale_norm(ln, gain, bias):
                    for u in SLOTS:
                        pool.wait_ge(ln_done[u], ln + 1)
                        link(nc.gpsimd.tensor_tensor(res[u][:], nrm[u][:], gain.unsqueeze(1).to_broadcast([P, TILES, D]), ALU.mult))
                        nc.gpsimd.tensor_tensor(res[u][:], res[u][:], bias.unsqueeze(1).to_broadcast([P, TILES, D]), ALU.add)\
                          .then_inc(res_ready[u], 1)

                norm_rstd(LN_XATTN)
                norm_rstd(LN_OUTER)
                for l in range(LAYERS):
                    def partners(t, u):
                        pool.wait_ge(sumsq_ready[u], TILES * l + t + 1)
                        halves = "p a (h s d) -> p (a h) s d"
                        src, dst = (v.rearrange(halves, s=2, d=DH // 2) for v in (raw[u], partner[u]))
                        for s in range(2):
                            for k in range(2):
                                heads = slice(HEADS * k, HEADS * k + HEADS)
                                factor = tab_b[:, l, t, k, s * DH // 2:(s + 1) * DH // 2]
                                last = nc.gpsimd.tensor_tensor(dst[:, heads, s, :], src[:, heads, 1 - s, :],
                                                               factor.unsqueeze(1).to_broadcast([P, HEADS, DH // 2]), ALU.mult)
                        last.then_inc(partner_ready[u], 1)
                        nc.gpsimd.tensor_scalar(rnorm[u][:, t, 0:HEADS], sumsq[u][:, t, 0:HEADS], 1e-24, 1.0 / DH, ALU.max, ALU.mult)
                        link(nc.gpsimd.tensor_scalar(rnorm[u][:, t, HEADS:], sumsq[u][:, t, HEADS:], 1e-24, None, ALU.max))
                        nc.gpsimd.tensor_tensor(rnorm[u][:, t, :], rnorm[u][:, t, :], neg_half[:], ALU.pow).then_inc(rnorm_ready[u], 1)

                    def normalise_k(t, u):
                        pool.wait_ge(turned_ready[u], TILES * l + t + 1)
                        pool.wait_ge(rnorm_ready[u], TILES * l + t + 1)
                        k = turned[u][:, 1, :].rearrange("p (h d) -> p h d", d=DH)
                        nc.gpsimd.tensor_tensor(k, k, rnorm[u][:, t, HEADS:].unsqueeze(2).to_broadcast([P, HEADS, DH]), ALU.mult)\
                          .then_inc(k_ready[u], 1)

                    for n in range(len(STEPS) + 1):
                        if n < len(STEPS):
                            partners(*STEPS[n])
                        if n >= 1:
                            normalise_k(*STEPS[n - 1])
                    for u in SLOTS:
                        pool.wait_ge(dve_emptied, dve_item["attn_out", l, TILES - 1, u] + 1)
                        add_bias(u, row("b2", l))
                    norm_rstd(LN_FF[l])
                norm_rstd(LN_TGT)
                for u in SLOTS:
                    pool.wait_ge(ln_done[u], LN_TGT + 1)
                    add_bias(u, row("sa_out_b"))
                norm_rstd(LN_1)
                scale_norm(LN_1, row("ln1_g"), res1_b[:])
                norm_rstd(LN_2)
                scale_norm(LN_2, row("ln2_g"), res2_b[:])
                norm_rstd(LN_3)
                scale_norm(LN_3, g3[:], b3[:])
                norm_rstd(LN_MOE)

            @block.sync
            def _(sp):
                def of_slot(dram, u):
                    return dram.rearrange("(i u) n d -> u i n d", u=len(SLOTS))[u][bass.ds(i_pass, 1)]

                for u in SLOTS:
                    sp.dma_start(ctx_t[u][:], of_slot(a["ctx"], u).rearrange("b (j p) d -> p (b j) d", p=CH))\
                      .then_inc(ctx_loaded[u], 16)
                    sp.dma_start(x[u][:], of_slot(a["x"], u).rearrange("b (t p) d -> p (b t) d", p=P))\
                      .then_inc(x_loaded[u], 16)
                half = D // 2
                for l in range(LAYERS):
                    for u in SLOTS:
                        sp.wait_ge(dve_emptied, dve_item["attn_out", l, TILES - 1, u] + 1)
                        sp.dma_start(shifted[u][:, :, 0:half], y[u][:, :, 0:half]).then_inc(shift_done[u], 16)
                        for lo, hi in ((0, 112), (112, P - 1)):
                            sp.dma_start(shifted[u][lo + 1:hi + 1, :, half:D], y[u][lo:hi, :, half:D]).then_inc(shift_done[u], 16)
                        sp.dma_start(shifted[u][0:1, 1:TILES, half:D], y[u][P - 1:P, 0:TILES - 1, half:D])\
                          .then_inc(shift_done[u], 16)
                for u in SLOTS:
                    sp.wait_ge(dve_emptied, dve_item["moe_out", u] + 1)
                    sp.dma_start(of_slot(out, u).rearrange("b (t p) d -> p (b t) d", p=P), y[u][:])\
                      .then_inc(x_stored[u], 16)
                for u in SLOTS:
                    sp.wait_ge(x_stored[u], 16)

        with nc.Fori(0, BATCH // len(SLOTS)) as i_pass:
            with nc.Block() as block:
                one_pass(i_pass, block)
            nc.all_engine_barrier(sems_to_clear=loop_sems)


def kernel(**inputs):
    import numpy as _np
    import concourse.bacc as _bacc
    from concourse import mybir as _mybir
    from ml_dtypes import bfloat16 as _bf16
    from concourse.bass_utils import run_bass_kernel_spmd as _run

    i = {k: _np.asarray(v) for k, v in inputs.items()}

    def column(*vs):
        out = []
        for v in vs:
            v = v.reshape(-1)
            n = -(-v.size // P) * P
            out.append(_np.concatenate([v, _np.zeros(n - v.size, v.dtype)]).reshape(-1, P).T)
        return _np.concatenate(out, 1)

    def spread(w):
        out = _np.zeros(w.shape[:-1] + (2, 4, 2 * CA_DH), w.dtype)
        out[..., :CA_DH] = w.reshape(w.shape[:-1] + (2, 4, CA_DH))
        return out.reshape(w.shape[:-1] + (2 * P,))

    def swap(v):
        return _np.concatenate([v[:, DH // 2:], v[:, :DH // 2]], 1)

    in_w, in_b = i["L1_xattn_in_proj_w"], i["L1_xattn_in_proj_b"]
    b1 = i["L0_ffn_b1"]
    cols = {
        "bq": [i["L0_xattn_bq"]], "bk": [i["L0_xattn_bk"]], "ln_g": list(i["L0_ffn_ln_g"]), "ln_b": list(i["L0_ffn_ln_b"]),
        "b1a": [b1[l, :HID] for l in range(LAYERS)], "b1g": [b1[l, HID:] for l in range(LAYERS)],
        "bv_sa": [i["L1_xattn_qkv_b"][2 * D:]], "ln1_g": [i["L1_xattn_ln1_g"]], "ln1_b": [i["L1_xattn_ln1_b"]],
        "ln2_g": [i["L1_xattn_ln2_g"]], "ln2_b": [i["L1_xattn_ln2_b"]], "bq_ca": [spread(in_b[:D])],
        "bk_ca": [spread(in_b[D:2 * D])], "lin1_b": [i["L1_xattn_lin1_b"]], "moe_b1": [i["L1_ffn_b1"]],
        "sb1": [i["L1_ffn_sb1"]], "sb2": list(i["L1_ffn_sb2"])}
    rows = {
        "gates": _np.concatenate([i["g_xattn"], i["g_ffn"]]), "bv": i["L0_xattn_bv"], "qs": i["L0_ffn_q_scale"],
        "ks": i["L0_ffn_k_scale"], "qs_swap": swap(i["L0_ffn_q_scale"]), "ks_swap": swap(i["L0_ffn_k_scale"]),
        "b2": i["L0_ffn_b2"], "bqk_sa": i["L1_xattn_qkv_b"][:2 * D], "sa_out_b": i["L1_xattn_sa_out_b"],
        "ln1_g": i["L1_xattn_ln1_g"], "ln1_b": i["L1_xattn_ln1_b"], "mha_out_b": i["L1_xattn_mha_out_b"],
        "ln2_g": i["L1_xattn_ln2_g"], "ln2_b": i["L1_xattn_ln2_b"], "lin2_b": i["L1_xattn_lin2_b"],
        "ln3_g": i["L1_xattn_ln3_g"], "ln3_b": i["L1_xattn_ln3_b"], "bv_ca": in_b[2 * D:],
        "router_b": i["L1_ffn_router_b"]}
    rot_a, rot_b = rotary_tables()
    arrays = {
        "x": i["x"], "ctx": i["ctx_1024"],
        "cols": _np.concatenate([column(*cols[n]) for n in COLS], 1),
        "rows": _np.concatenate([rows[n].reshape(-1) for n in ROWS])[None, :],
        "ident": _np.eye(P, dtype=_np.float32), "rot_a": rot_a, "rot_b": rot_b, "masks": band_masks(), 
        "sel": expert_selector().astype(_bf16), "identb": _np.eye(P).astype(_bf16),
        "wq": i["L0_xattn_Wq"], "wk": i["L0_xattn_Wk"], "wv": i["L0_xattn_Wv"],
        "wqkv": i["L0_ffn_wqkv"], "wo": i["L0_ffn_wo"], "w1": i["L0_ffn_w1"], "w2": i["L0_ffn_w2"],
        "w_sa": i["L1_xattn_qkv_w"].T, "w_sao": i["L1_xattn_sa_out_w"].T, "w_caq": spread(in_w[:D].T),
        "w_cak": spread(in_w[D:2 * D].T), "w_cav": in_w[2 * D:].T, "w_cao": i["L1_xattn_mha_out_w"].T,
        "w_l1": i["L1_xattn_lin1_w"].T, "w_l2": i["L1_xattn_lin2_w"].T, "w_rt": i["L1_ffn_router_w"],
        "w_m1": i["L1_ffn_w1"].transpose(1, 0, 2).reshape(D, EXPERTS * EXP_H), "b_m2": i["L1_ffn_b2"],
        "w_m2": i["L1_ffn_w2"].reshape(EXPERTS * EXP_H, D), "w_s1": i["L1_ffn_sw1"], "w_s2": i["L1_ffn_sw2"]}
    nc = _bacc.Bacc("TRN2", target_bir_lowering=False, num_devices=1)
    aps, fed = {}, {}
    for name, v in arrays.items():
        v = _np.ascontiguousarray(v)
        fed[f"in_{name}_dram"] = v
        aps[name] = nc.dram_tensor(f"in_{name}_dram", v.shape, _mybir.dt.from_np(v.dtype), kind="ExternalInput").ap()
    out = nc.dram_tensor("out_0_dram", (BATCH, SEQ, D), _mybir.dt.float32, kind="ExternalOutput").ap()
    build(nc, aps, out)
    r = _run(nc, [fed], core_ids=[0])
    return r.results[0]["out_0_dram"]
```

```python
from contextlib import ExitStack

import numpy as np

import concourse.bass as bass
from concourse import mybir

ALU = mybir.AluOpType
ACT = mybir.ActivationFunctionType
AX = mybir.AxisListType
F32 = mybir.dt.float32
BF16 = mybir.dt.bfloat16

BATCH, SEQ, D = 4, 512, 128
P = 128
TILES = SEQ // P
SLOTS = (0, 1)
CTX = 154
CH = CTX // 2
LAYERS, HEADS, DH, WINDOW = 2, 8, 64, 64
INNER = HEADS * DH
KEYS = P + WINDOW
HID = int(D * 4 * 2 / 3)
HID_W = [min(P, HID - m * P) for m in range(-(-HID // P))]
CA_HEADS, CA_DH = 8, 16
FF = 512
EXPERTS, TOPK, EXP_H = 64, 8, 32
ROUTED = EXPERTS * EXP_H // P
SHARED = 4
EPS = 1e-5
MASKED = -1.0e30
LOWEST = -3.0e38
ACT_BANKS, DVE_BANKS = 3, 4
HALF = HEADS // 2

LN_XATTN, LN_OUTER, LN_FF, LN_TGT, LN_1, LN_2, LN_3, LN_MOE = 0, 1, (2, 3), 4, 5, 6, 7, 8
CHUNKS = ROUTED + SHARED
PER_STEP = 2

STEPS = 8 + LAYERS * (1 + 2 * TILES + 1 + 2 * TILES + 2 + 5) + 7 + 2 * TILES + 2 + 7 + 4 + (CHUNKS + 2) // PER_STEP + 1
LEAD = 14
TOGETHER = 8
TURNS = [0, 1] * TOGETHER + [0, 0, 1] * LEAD + [0, 1] * (STEPS - TOGETHER - 2 * LEAD) + [1] * LEAD

SM_FIRST = 0


def sm_local(l, t):
    return 1 + TILES * l + t


def sm_cross(t):
    return 1 + TILES * LAYERS + t


def half_done(number, g):
    return 2 * number + g


def layout(names):
    at, out = 0, {}
    for name, w in names:
        out[name] = (at, w)
        at += w
    return out, at


COLS, N_COLS = layout([
    ("bq", 1), ("bk", 1), ("ln_g", 2), ("ln_b", 2), ("b1a", 6), ("b1g", 6), ("bv_sa", 1),
    ("ln1_g", 1), ("ln1_b", 1), ("ln2_g", 1), ("ln2_b", 1), ("bq_ca", 2), ("bk_ca", 2),
    ("lin1_b", 4), ("moe_b1", ROUTED), ("sb1", SHARED), ("sb2", 2)])
ROWS, N_ROWS = layout([
    ("gates", 4), ("bv", D), ("qs", 2 * DH), ("ks", 2 * DH), 
    ("b2", 2 * D), ("bqk_sa", 2 * D), ("sa_out_b", D), ("ln1_g", D), ("ln1_b", D), ("mha_out_b", D),
    ("ln2_g", D), ("ln2_b", D), ("lin2_b", D), ("ln3_g", D), ("ln3_b", D), ("bv_ca", 2 * D),
    ("router_b", EXPERTS)])
GX0, GX1, GF0, GF1 = range(4)


def rotary_tables():
    f = np.float32
    half = np.arange(0, DH, 2, dtype=f)
    inv_freq = (f(1.0) / np.power(f(10000.0), half / f(DH))).astype(f)
    t = np.arange(SEQ, dtype=f)
    freqs = (t[:, None] * inv_freq[None, :]).astype(f)
    base = ((half + f(0.4 * DH)) / f(1.4 * DH)).astype(f)
    power = ((t - f(SEQ // 2)) / f(WINDOW // 2)).astype(f)
    scale = np.power(base[None, :], power[:, None]).astype(f)
    cos, sin = np.cos(freqs), np.sin(freqs)
    root = f(DH ** 0.5)
    a = np.stack([np.concatenate([cos * scale] * 2, -1), np.concatenate([cos / scale * root] * 2, -1)], 1)
    b = np.stack([np.concatenate([sin * scale, -sin * scale], -1), np.concatenate([sin / scale * root, -sin / scale * root], -1)], 1)
    shape = (TILES, P, 2, DH)
    return [np.ascontiguousarray(x.astype(f).reshape(shape).transpose(1, 0, 2, 3).reshape(P, -1)) for x in (a, b)]


def band_masks():
    i = np.arange(P)[:, None]
    j = np.arange(KEYS)[None, :] - WINDOW
    band = np.where((j <= i) & (j >= i - WINDOW), 0.0, MASKED)
    first = np.where(j < 0, MASKED, band)
    return np.stack([first, band], 1).reshape(P, 2 * KEYS).astype(np.float32)


def expert_selector():
    sel = np.zeros((EXPERTS, ROUTED, P), np.float32)
    for c in range(ROUTED):
        for j in range(P):
            sel[c * (P // EXP_H) + j // EXP_H, c, j] = 1.0
    return np.concatenate([sel, sel], 0).reshape(2 * EXPERTS, ROUTED * P)


def build(nc, a, out):
    ctx = ExitStack()
    with ctx:
        def sb(name, shape, dt=F32):
            return ctx.enter_context(nc.sbuf_tensor(name, shape, dt))

        def per_slot(name, shape, dt=F32):
            return [sb(f"{name}{u}", shape, dt) for u in SLOTS]

        def sem(name):
            return ctx.enter_context(nc.semaphore(name))

        cols = sb("cols", [P, N_COLS])
        rows = sb("rows", [P, N_ROWS])
        ident = sb("ident", [P, P])
        identb = sb("identb", [P, P], BF16)
        masks = sb("masks", [P, 2, KEYS])
        no_mask = sb("no_mask", [P, CTX])
        sel = sb("sel", [P, ROUTED, P], BF16)
        neg_half = sb("neg_half", [P, 2 * HEADS])
        gate = sb("gate", [P, 4])
        wq, wk, wv = (sb(n, [P, D]) for n in ("wq", "wk", "wv"))
        wqkv = sb("wqkv", [P, LAYERS, 3 * INNER])
        wo = sb("wo", [P, LAYERS, INNER // P, D])
        w1 = sb("w1", [P, LAYERS, 2 * HID])
        w2 = sb("w2", [P, LAYERS, len(HID_W), D])
        w_sa = sb("w_sa", [P, 3 * D])
        w_sao = sb("w_sao", [P, D])
        w_caq = sb("w_caq", [P, 2, P])
        w_cak = sb("w_cak", [P, 2, P])
        w_cav = sb("w_cav", [P, 2 * D])
        w_cao = sb("w_cao", [P, 2, D])
        w_l1 = sb("w_l1", [P, FF])
        w_l2 = sb("w_l2", [P, FF // P, D])
        w_rt = sb("w_rt", [P, EXPERTS])
        w_m1 = sb("w_m1", [P, ROUTED * P])
        w_m2 = sb("w_m2", [P, ROUTED, D])
        w_s1 = sb("w_s1", [P, SHARED, P])
        w_s2 = sb("w_s2", [P, SHARED, D])
        b_m2 = sb("b_m2", [EXPERTS, D])
        tab_a = sb("tab_a", [P, LAYERS, TILES, 2, DH])
        tab_b = sb("tab_b", [P, LAYERS, TILES, 2, DH])
        res1_b = sb("res1_b", [P, D])
        res2_b = sb("res2_b", [P, D])
        g3 = sb("g3", [P, D])
        b3 = sb("b3", [P, D])
        sb2_sum = sb("sb2_sum", [P, 1])
        sb2_g = sb("sb2_g", [P, 1])

        x = per_slot("x", [P, TILES, D])
        y = per_slot("y", [P, TILES, D])
        res = per_slot("res", [P, TILES, D])
        nrm = per_slot("nrm", [P, TILES, D])
        shifted = per_slot("shifted", [P, TILES, D])
        stats = per_slot("stats", [P, TILES, 6])
        mv = per_slot("mv", [P, TILES, 2])
        rstd = per_slot("rstd", [P, TILES])
        ctx_t = per_slot("ctx_t", [CH, 2, D])
        ctxT = per_slot("ctxT", [P, CTX])
        hT = per_slot("hT", [P, SEQ])
        hTs = per_slot("hTs", [P, WINDOW + SEQ])
        qT = per_slot("qT", [P, INNER // P, SEQ])
        kT = per_slot("kT", [P, INNER // P, WINDOW + SEQ])
        kcT = per_slot("kcT", [P, 2, CTX])
        v_loc = per_slot("v_loc", [P, TILES + 1, INNER])
        work = per_slot("work", [P, 3 * 2 * INNER])
        ptb = per_slot("ptb", [P, HEADS, P])
        oT = [h[:].rearrange("p (c q) -> p c q", q=P) for h in hT]
        peak = per_slot("peak", [P, HEADS])
        nbias = per_slot("nbias", [P, HEADS])
        sums = per_slot("sums", [P, HEADS])
        rinv = per_slot("rinv", [P, HEADS])
        sumsq = per_slot("sumsq", [P, TILES, 2 * HEADS])
        rnorm = per_slot("rnorm", [P, TILES, 2 * HEADS])
        diag = per_slot("diag", [P, 4, TILES])
        W2 = 2 * INNER
        rot_a, rot_b = (work[0][:, k * 512:(k + 1) * 512].rearrange("p (t a d) -> p t a d", t=TILES, a=2) for k in range(2))
        raw = [w[:, 0:W2].rearrange("p (a n) -> p a n", a=2) for w in work]
        partner = [w[:, W2:2 * W2].rearrange("p (a n) -> p a n", a=2) for w in work]
        turned = [w[:, 2 * W2:3 * W2].rearrange("p (a n) -> p a n", a=2) for w in work]
        prob = [w[:, 0:HEADS * KEYS].rearrange("p (h k) -> p h k", h=HEADS) for w in work]
        pta = [w[:, 1536:2560].rearrange("p (h q) -> p h q", h=HEADS) for w in work]
        v_ctx = [w[0:CH, 2560:3072].rearrange("p (j n) -> p j n", j=2) for w in work]
        gel = [w[:, 0:3 * SEQ].rearrange("p (m n) -> p m n", m=3) for w in work]
        hid = [w[:, 0:3 * SEQ].rearrange("p (m n) -> p m n", m=3) for w in work]
        weighed = [w[:, 3 * SEQ:6 * SEQ].rearrange("p (m n) -> p m n", m=3) for w in work]
        def route_view(u, k, n):
            return v_loc[u][:, k, 0:n]
        logit = [route_view(u, 0, 256).rearrange("p (t e) -> p t e", t=TILES) for u in SLOTS]
        expw = [route_view(u, 1, 256).rearrange("p (t e) -> p t e", t=TILES) for u in SLOTS]
        rest = [route_view(u, 2, 256).rearrange("p (t e) -> p t e", t=TILES) for u in SLOTS]
        cw = [route_view(u, 3, 256).rearrange("p (t e) -> p t e", t=TILES) for u in SLOTS]
        cwT = [v_loc[u][0:EXPERTS, 4, :] for u in SLOTS]
        top = per_slot("top", [P, TILES, TOPK])
        rsmall = per_slot("rsmall", [P, 3, TILES])
        cw_hm = [v_loc[u][:, 0, 256:512].bitcast(BF16).rearrange("p (t e) -> p t e", t=TILES) for u in SLOTS]
        cw_lo = [v_loc[u][:, 1, 256:384].bitcast(BF16).rearrange("p (t e) -> p t e", t=TILES) for u in SLOTS]
        cwT_hm = [v_loc[u][:, 2, 256:512].bitcast(BF16) for u in SLOTS]
        cwT_lo = [v_loc[u][0:EXPERTS, 3, 256:512].bitcast(BF16) for u in SLOTS]

        def flat(t):
            return t[:].rearrange("p t d -> p (t d)")

        def col(name, k=0, n=P):
            at, _ = COLS[name]
            return cols[0:n, at + k:at + k + 1]

        def row(name, k=0, w=D, n=P):
            at, _ = ROWS[name]
            return rows[0:n, at + k * w:at + k * w + w]

        act_psum = [ctx.enter_context(nc.psum_tensor(f"act_psum{i}", [P, 512], F32)) for i in range(ACT_BANKS)]
        dve_psum = [ctx.enter_context(nc.psum_tensor(f"dve_psum{i}", [P, 512], F32)) for i in range(DVE_BANKS)]
        moe_psum = ctx.enter_context(nc.psum_tensor("moe_psum", [P, 512], F32))

        small_loaded = sem("small_loaded")
        w_loaded = {k: sem(f"{k}_loaded") for k in ("first", "local", "cross", "moe")}
        set_up = sem("set_up")
        gate_made = sem("gate_made")
        pool_setup = sem("pool_setup")

        loop_sem_numbers = []

        def loop_sem(name):
            s = sem(name)
            loop_sem_numbers.append(s.num)
            return s

        def slot_sems(name):
            return [loop_sem(f"{name}{u}") for u in SLOTS]

        act_filled, act_emptied = loop_sem("act_filled"), loop_sem("act_emptied")
        dve_filled, dve_emptied = loop_sem("dve_filled"), loop_sem("dve_emptied")
        act_chain, dve_chain, pool_chain = loop_sem("act_chain"), loop_sem("dve_chain"), loop_sem("pool_chain")
        x_loaded, ctx_loaded = slot_sems("x_loaded"), slot_sems("ctx_loaded")
        ln_stats, ln_rstd, ln_done = slot_sems("ln_stats"), slot_sems("ln_rstd"), slot_sems("ln_done")
        peak_ready, exp_done = slot_sems("peak_ready"), slot_sems("exp_done")
        probs_lo_ready, probs_hi_ready = slot_sems("probs_lo_ready"), slot_sems("probs_hi_ready")
        sq_ready, sumsq_ready, rnorm_ready = slot_sems("sq_ready"), slot_sems("sumsq_ready"), slot_sems("rnorm_ready")
        partner_ready, turned_ready, k_ready = slot_sems("partner_ready"), slot_sems("turned_ready"), slot_sems("k_ready")
        own_ready, rinv_ready = slot_sems("own_ready"), slot_sems("rinv_ready")
        res_ready, shift_done = slot_sems("res_ready"), slot_sems("shift_done")
        diag_ready, diag_exp = slot_sems("diag_ready"), slot_sems("diag_exp")
        logit_ready, expw_ready, cw_ready = slot_sems("logit_ready"), slot_sems("expw_ready"), slot_sems("cw_ready")
        moe_filled, moe_emptied = loop_sem("moe_filled"), loop_sem("moe_emptied")
        x_stored = slot_sems("x_stored")

        with nc.Block() as block:
            @block.sync
            def _(sp):
                for dst, src in ((rows[:], a["rows"].to_broadcast([P, N_ROWS])), (cols[:], a["cols"]), (ident[:], a["ident"]),
                                 (work[0][:, 0:512], a["rot_a"]), (work[0][:, 512:1024], a["rot_b"]),
                                 (masks[:].rearrange("p m k -> p (m k)"), a["masks"]), (sel[:].rearrange("p c n -> p (c n)"), a["sel"]), (identb[:], a["identb"])):
                    sp.dma_start(dst, src).then_inc(small_loaded, 16)
                for dst, src in ((wk[:], a["wk"]), (wv[:], a["wv"]), (wq[:], a["wq"])):
                    sp.dma_start(dst, src).then_inc(w_loaded["first"], 16)
                sp.dma_start(wqkv[:], a["wqkv"].rearrange("l p n -> p l n")).then_inc(w_loaded["local"], 16)
                sp.dma_start(wo[:].rearrange("p l c n -> p (l c) n"),
                             a["wo"].rearrange("l (c p) n -> p (l c) n", p=P)).then_inc(w_loaded["local"], 16)
                sp.dma_start(w1[:], a["w1"].rearrange("l p n -> p l n")).then_inc(w_loaded["local"], 16)
                for m, w in enumerate(HID_W):
                    sp.dma_start(w2[0:w, :, m, :], a["w2"][:, m * P:m * P + w, :].rearrange("l p n -> p l n"))\
                      .then_inc(w_loaded["local"], 16)
                for dst, src in ((w_sa[:], a["w_sa"]), (w_sao[:], a["w_sao"]),
                                 (w_caq[:].rearrange("p c n -> p (c n)"), a["w_caq"]),
                                 (w_cak[:].rearrange("p c n -> p (c n)"), a["w_cak"]),
                                 (w_cav[:], a["w_cav"]), (w_cao[:], a["w_cao"]), (w_l1[:], a["w_l1"]),
                                 (w_l2[:], a["w_l2"].rearrange("(c p) n -> p c n", p=P))):
                    sp.dma_start(dst, src).then_inc(w_loaded["cross"], 16)
                for dst, src in ((w_rt[:], a["w_rt"]), (b_m2[:], a["b_m2"]), (w_m1[:], a["w_m1"]),
                                 (w_m2[:], a["w_m2"].rearrange("(c p) n -> p c n", p=P)),
                                 (w_s1[:].rearrange("p (e c) n -> p e (c n)", e=2), a["w_s1"].rearrange("e p n -> p e n")),
                                 (w_s2[:].rearrange("p (e c) n -> p e c n", e=2),
                                  a["w_s2"].rearrange("e (c p) n -> p e c n", p=P))):
                    sp.dma_start(dst, src).then_inc(w_loaded["moe"], 16)

            @block.scalar
            def _(act):
                act.wait_ge(small_loaded, 8 * 16)
                at, _ = ROWS["gates"]
                nc.scalar.activation(gate[:], rows[:, at:at + 4], ACT.Tanh).then_inc(gate_made, 1)

            @block.vector
            def _(dve):
                nc.vector.memset(no_mask[:], 0.0)
                nc.vector.memset(neg_half[:], -0.5)
                for u in SLOTS:
                    nc.vector.memset(hTs[u][:, 0:WINDOW], 0.0)
                    nc.vector.memset(hTs[u][D // 2:D, WINDOW:WINDOW + 1], 0.0)
                    nc.vector.memset(kT[u][:, :, 0:WINDOW], 0.0)
                    nc.vector.memset(shifted[u][0:1, 0, D // 2:D], 0.0)
                dve.wait_ge(small_loaded, 8 * 16)
                nc.vector.tensor_tensor(res1_b[:], row("ln1_b"), row("mha_out_b"), ALU.add)
                nc.vector.tensor_tensor(res2_b[:], row("ln2_b"), row("lin2_b"), ALU.add)
                nc.vector.tensor_tensor(sb2_sum[:], col("sb2", 0), col("sb2", 1), ALU.add).then_inc(set_up, 1)
                dve.wait_ge(gate_made, 1)
                nc.vector.tensor_scalar(g3[:], row("ln3_g"), gate[:, GX1:GX1 + 1], None, ALU.mult)
                nc.vector.tensor_scalar(b3[:], row("ln3_b"), gate[:, GX1:GX1 + 1], None, ALU.mult)
                dve.wait_ge(set_up, 1)
                nc.vector.tensor_scalar(sb2_g[:], sb2_sum[:], gate[:, GF1:GF1 + 1], None, ALU.mult).then_inc(set_up, 1)
                dve.wait_ge(set_up, 2)

            @block.gpsimd
            def _(pool):
                pool.wait_ge(small_loaded, 8 * 16)
                for l in range(LAYERS):
                    for k, name in enumerate(("qs", "ks")):
                        for tab, rot in ((tab_a, rot_a), (tab_b, rot_b)):
                            last = nc.gpsimd.tensor_tensor(
                                tab[:, l, :, k, :], rot[:, :, k, :],
                                row(name, l, DH).unsqueeze(1).to_broadcast([P, TILES, DH]), ALU.mult)
                last.then_inc(pool_setup, 1)
                pool.wait_ge(pool_setup, 1)

        loop_sems = range(min(loop_sem_numbers), max(loop_sem_numbers) + 1)

        def one_pass(i_pass, block):
            act_item, dve_item = {}, {}

            def in_turn(slot_steps):
                steps = [slot_steps(u) for u in SLOTS]
                for u in TURNS:
                    next(steps[u])
                assert all(next(step, "done") == "done" for step in steps)

            @block.tensor
            def _(pe):
                def act_bank(name):
                    n = len(act_item)
                    act_item[name] = n
                    if n >= ACT_BANKS:
                        pe.wait_ge(act_emptied, n - ACT_BANKS + 1)
                    return act_psum[n % ACT_BANKS]

                def dve_bank(name):
                    n = len(dve_item)
                    dve_item[name] = n
                    if n >= DVE_BANKS:
                        pe.wait_ge(dve_emptied, n - DVE_BANKS + 1)
                    return dve_psum[n % DVE_BANKS]

                def transpose_tiles(name, src, u):
                    bank = act_bank(name)
                    for t in range(TILES):
                        last = nc.tensor.transpose(bank[:, t * P:(t + 1) * P], src[u][:, t, :], ident[:])
                    last.then_inc(act_filled, 1)

                def transpose_norm(name, ln, u):
                    pe.wait_ge(ln_done[u], ln + 1)
                    transpose_tiles(name, nrm, u)

                def local_attention_steps(l, u):
                    attn_w = wqkv[:, l, :]

                    def project_qk(t):
                        h = hTs[u][:, WINDOW + t * P:WINDOW + (t + 1) * P]
                        for k in range(2):
                            bank = act_bank(("qk", l, t, u, k))
                            nc.tensor.matmul(bank[:], h, attn_w[:, k * INNER:(k + 1) * INNER], start=True, stop=True)\
                              .then_inc(act_filled, 1)

                    def project_v(j):
                        n = P if j < TILES else WINDOW
                        bank = act_bank(("v_loc", l, j, u))
                        nc.tensor.matmul(bank[0:n, :], hTs[u][:, j * P:j * P + n], attn_w[:, 2 * INNER:3 * INNER],
                                         start=True, stop=True).then_inc(act_filled, 1)

                    def turn(t, u):
                        pe.wait_ge(turned_ready[u], TILES * l + t + 1)
                        bank = act_bank(("qT", l, t, u))
                        for c in range(INNER // P):
                            last = nc.tensor.transpose(bank[:, c * P:(c + 1) * P], turned[u][:, 0, c * P:(c + 1) * P], ident[:])
                        last.then_inc(act_filled, 1)
                        pe.wait_ge(k_ready[u], TILES * l + t + 1)
                        bank = dve_bank(("kT", l, t, u))
                        for c in range(INNER // P):
                            last = nc.tensor.transpose(bank[:, c * P:(c + 1) * P], turned[u][:, 1, c * P:(c + 1) * P], ident[:])
                        last.then_inc(dve_filled, 1)

                    def scores(t, u):
                        if t == 0:
                            pe.wait_ge(act_emptied, act_item["qT", l, TILES - 1, u] + 1)
                            pe.wait_ge(dve_emptied, dve_item["kT", l, TILES - 1, u] + 1)
                        for g in range(2):
                            for odd in range(2):
                                bank = dve_bank(("s_local", l, t, u, g, odd))
                                for i in range(2):
                                    c = 2 * g + i
                                    half = slice(DH * odd, DH * odd + DH)
                                    last = nc.tensor.matmul(bank[:, i * KEYS:(i + 1) * KEYS], qT[u][half, c, t * P:(t + 1) * P],
                                                            kT[u][half, c, t * P:t * P + KEYS], start=True, stop=True)
                                last.then_inc(dve_filled, 1)

                    def turn_probs(t, u):
                        for g in range(2):
                            pe.wait_ge((probs_lo_ready, probs_hi_ready)[g][u], sm_local(l, t))
                            bank = dve_bank(("pta", l, t, u, g))
                            for i in range(4):
                                last = nc.tensor.transpose(bank[:, i * P:(i + 1) * P], prob[u][:, 4 * g + i, 0:P], ident[:])
                            last.then_inc(dve_filled, 1)
                            bank = act_bank(("ptb", l, t, u, g))
                            for i in range(4):
                                last = nc.tensor.transpose(bank[0:WINDOW, i * P:(i + 1) * P], prob[u][:, 4 * g + i, P:KEYS], ident[:])
                            last.then_inc(act_filled, 1)

                    def mix_values(t, u):
                        pe.wait_ge(dve_emptied, dve_item["pta", l, t, u, 1] + 1)
                        pe.wait_ge(act_emptied, act_item["ptb", l, t, u, 1] + 1)
                        bank = act_bank(("oT", l, t, u))
                        for h in range(HEADS):
                            f = slice(h * DH, (h + 1) * DH)
                            dst = bank[h % 2 * DH:(h % 2 + 1) * DH, h // 2 * P:(h // 2 + 1) * P]
                            nc.tensor.matmul(dst, v_loc[u][:, t, f], pta[u][:, h, :], start=True, stop=False)
                            last = nc.tensor.matmul(dst, v_loc[u][0:WINDOW, t + 1, f], ptb[u][0:WINDOW, h, :], start=False, stop=True)
                        last.then_inc(act_filled, 1)

                    def project_out(t, u):
                        pe.wait_ge(act_emptied, act_item["oT", l, t, u] + 1)
                        bank = dve_bank(("attn_out", l, t, u))
                        for c in range(INNER // P):
                            last = nc.tensor.matmul(bank[:, 0:D], oT[u][:, c, :], wo[:, l, c, :],
                                                    start=(c == 0), stop=(c == INNER // P - 1))
                        last.then_inc(dve_filled, 1)

                    pe.wait_ge(act_emptied, act_item["hTs", l, u] + 1)
                    for t in range(TILES):
                        project_qk(t)
                        if t >= 1:
                            turn(t - 1, u)
                        yield
                        project_v(t)
                        if t == TILES - 1:
                            project_v(TILES)
                        yield
                    turn(TILES - 1, u)
                    yield
                    for n in range(TILES + 1):
                        if n >= 1:
                            mix_values(n - 1, u)
                        if n < TILES:
                            scores(n, u)
                        yield
                        if n >= 1:
                            project_out(n - 1, u)
                        if n < TILES:
                            turn_probs(n, u)
                        yield

                def cross_attention_steps(u):
                    def ca_scores(t, u):
                        if t == 0:
                            pe.wait_ge(act_emptied, act_item["q_ca", u, 1] + 1)
                        for j in range(4):
                            bank = dve_bank(("s_ca", t, u, j))
                            for c in range(2):
                                part = slice(32 * j, 32 * j + 32)
                                last = nc.tensor.matmul(bank[:, c * CTX:(c + 1) * CTX], qT[u][part, c, t * P:(t + 1) * P],
                                                        kcT[u][part, c, :], start=True, stop=True)
                            last.then_inc(dve_filled, 1)

                    def ca_turn_probs(t, u):
                        for g in range(2):
                            pe.wait_ge((probs_lo_ready, probs_hi_ready)[g][u], sm_cross(t))
                            for j, bank, filled in ((0, dve_bank(("pta_ca", t, u, g)), dve_filled),
                                                    (1, act_bank(("ptb_ca", t, u, g)), act_filled)):
                                for i in range(4):
                                    last = nc.tensor.transpose(bank[0:CH, i * P:(i + 1) * P],
                                                               prob[u][:, 4 * g + i, j * CH:(j + 1) * CH], ident[:])
                                last.then_inc(filled, 1)

                    def ca_mix(t, u):
                        pe.wait_ge(dve_emptied, dve_item["pta_ca", t, u, 1] + 1)
                        pe.wait_ge(act_emptied, act_item["ptb_ca", t, u, 1] + 1)
                        bank = act_bank(("oT_ca", t, u))
                        for h in range(CA_HEADS):
                            j, c = divmod(h, 2)
                            part = slice(32 * j, 32 * j + 32)
                            v = slice(c * P + 32 * j, c * P + 32 * j + 32)
                            for k, pt in enumerate((pta, ptb)):
                                last = nc.tensor.matmul(bank[part, c * P:(c + 1) * P], v_ctx[u][:, k, v], pt[u][0:CH, h, :],
                                                        start=(k == 0), stop=(k == 1))
                        last.then_inc(act_filled, 1)

                    def ca_project_out(t, u):
                        pe.wait_ge(act_emptied, act_item["oT_ca", t, u] + 1)
                        bank = dve_bank(("ca_out", t, u))
                        for c in range(2):
                            last = nc.tensor.matmul(bank[:, 0:D], oT[u][:, c, :], w_cao[:, c, :], start=(c == 0), stop=(c == 1))
                        last.then_inc(dve_filled, 1)

                    for n in range(TILES + 1):
                        if n >= 1:
                            ca_mix(n - 1, u)
                        if n < TILES:
                            ca_scores(n, u)
                        yield
                        if n >= 1:
                            ca_project_out(n - 1, u)
                        if n < TILES:
                            ca_turn_probs(n, u)
                        yield

                def expert_hidden(u, c):
                    bank = act_bank(("moe_h", u, c))
                    w = w_m1[:, c * P:(c + 1) * P] if c < ROUTED else w_s1[:, c - ROUTED, :]
                    nc.tensor.matmul(bank[:], w, hT[u][:], start=True, stop=True).then_inc(act_filled, 1)
                    if c < ROUTED:
                        if c == 0:
                            pe.wait_ge(dve_emptied, dve_item["cwT_lo", u] + 1)
                        bank = dve_bank(("moe_w", u, c))
                        nc.tensor.matmul(bank[:], sel[:, c, :], cwT_hm[u], start=True, stop=False)
                        nc.tensor.matmul(bank[:], sel[0:EXPERTS, c, :], cwT_lo[u], start=False, stop=True)\
                          .then_inc(dve_filled, 1)

                def expert_out(u, c):
                    if c < ROUTED:
                        pe.wait_ge(dve_emptied, dve_item["moe_w", u, c] + 1)
                    else:
                        pe.wait_ge(act_emptied, act_item["moe_h", u, c] + 1)
                    if c == 0 and u > 0:
                        pe.wait_ge(moe_emptied, u)
                    w = w_m2[:, c, :] if c < ROUTED else w_s2[:, c - ROUTED, :]
                    nc.tensor.matmul(moe_psum[:], w, weighed[u][:, c % 3, :], start=(c == 0), stop=False)

                def slot_steps(u):
                    if u == 0:
                        pe.wait_ge(w_loaded["first"], 3 * 16)
                    pe.wait_ge(ctx_loaded[u], 16)
                    bank = act_bank(("ctxT", u))
                    for j in range(2):
                        last = nc.tensor.transpose(bank[:, j * CH:(j + 1) * CH], ctx_t[u][:, j, :], ident[0:CH, 0:CH])
                    last.then_inc(act_filled, 1)
                    yield
                    pe.wait_ge(act_emptied, act_item["ctxT", u] + 1)
                    bank = act_bank(("k", u))
                    nc.tensor.matmul(bank[:, 0:CTX], wk[:], ctxT[u][:], start=True, stop=True).then_inc(act_filled, 1)
                    bank = dve_bank(("v", u))
                    for j in range(2):
                        last = nc.tensor.matmul(bank[0:CH, j * D:(j + 1) * D], ctxT[u][:, j * CH:(j + 1) * CH], wv[:],
                                                start=True, stop=True)
                    last.then_inc(dve_filled, 1)
                    yield
                    transpose_norm(("hT_first", u), LN_XATTN, u)
                    yield
                    pe.wait_ge(act_emptied, act_item["hT_first", u] + 1)
                    bank = act_bank(("q", u))
                    nc.tensor.matmul(bank[:], wq[:], hT[u][:], start=True, stop=True).then_inc(act_filled, 1)
                    yield
                    pe.wait_ge(act_emptied, act_item["q", u] + 1)
                    for t in range(TILES):
                        bank = dve_bank(("s_first", u, t))
                        nc.tensor.matmul(bank[:, 0:CTX], qT[u][:, 0, t * P:(t + 1) * P], kcT[u][:, 0, :],
                                         start=True, stop=True).then_inc(dve_filled, 1)
                    yield
                    pe.wait_ge(exp_done[u], SM_FIRST + 1)
                    for j, bank in ((0, dve_bank(("pt_first", u))), (1, act_bank(("pt_first", u)))):
                        for t in range(TILES):
                            last = nc.tensor.transpose(bank[0:CH, t * P:(t + 1) * P],
                                                       prob[u][:, t, j * CH:(j + 1) * CH], ident[:])
                        last.then_inc(dve_filled if j == 0 else act_filled, 1)
                    yield
                    pe.wait_ge(dve_emptied, dve_item["pt_first", u] + 1)
                    pe.wait_ge(act_emptied, act_item["pt_first", u] + 1)
                    bank = dve_bank(("o_first", u))
                    for t in range(TILES):
                        for j, pt in enumerate((pta, ptb)):
                            last = nc.tensor.matmul(bank[:, t * D:(t + 1) * D], pt[u][0:CH, t, :], v_ctx[u][:, j, 0:D],
                                                    start=(j == 0), stop=(j == 1))
                    last.then_inc(dve_filled, 1)
                    yield
                    yield

                    if u == 0:
                        pe.wait_ge(w_loaded["local"], 6 * 16)
                    for l in range(LAYERS):
                        if l == 0:
                            pe.wait_ge(ln_done[u], LN_OUTER + 1)
                        else:
                            pe.wait_ge(dve_emptied, dve_item["ff_out", l - 1, u] + 1)
                        transpose_tiles(("hTs", l, u), y, u)
                        yield
                        yield from local_attention_steps(l, u)
                        yield
                        yield
                        transpose_norm(("hT_ff", l, u), LN_FF[l], u)
                        yield
                        pe.wait_ge(act_emptied, act_item["hT_ff", l, u] + 1)
                        for m, w in enumerate(HID_W):
                            bank = act_bank(("ff_g", l, m, u))
                            nc.tensor.matmul(bank[0:w, :], w1[:, l, HID + m * P:HID + m * P + w], hT[u][:],
                                             start=True, stop=True).then_inc(act_filled, 1)
                            bank = dve_bank(("ff_a", l, m, u))
                            nc.tensor.matmul(bank[0:w, :], w1[:, l, m * P:m * P + w], hT[u][:],
                                             start=True, stop=True).then_inc(dve_filled, 1)
                        yield
                        pe.wait_ge(dve_emptied, dve_item["ff_a", l, len(HID_W) - 1, u] + 1)
                        bank = dve_bank(("ff_out", l, u))
                        for t in range(TILES):
                            for m, w in enumerate(HID_W):
                                last = nc.tensor.matmul(bank[:, t * D:(t + 1) * D], qT[u][0:w, m, t * P:(t + 1) * P],
                                                        w2[0:w, l, m, :], start=(m == 0), stop=(m == len(HID_W) - 1))
                        last.then_inc(dve_filled, 1)
                        yield

                    if u == 0:
                        pe.wait_ge(w_loaded["cross"], 8 * 16)
                    bank = act_bank(("kc", u))
                    for c in range(2):
                        last = nc.tensor.matmul(bank[:, c * CTX:(c + 1) * CTX], w_cak[:, c, :], ctxT[u][:], start=True, stop=True)
                    last.then_inc(act_filled, 1)
                    bank = dve_bank(("vc", u))
                    for j in range(2):
                        last = nc.tensor.matmul(bank[0:CH, 2 * D * j:2 * D * (j + 1)], ctxT[u][:, j * CH:(j + 1) * CH], w_cav[:],
                                                start=True, stop=True)
                    last.then_inc(dve_filled, 1)
                    yield
                    pe.wait_ge(ln_done[u], LN_TGT + 1)
                    transpose_tiles(("hT_sa", u), y, u)
                    yield
                    pe.wait_ge(act_emptied, act_item["hT_sa", u] + 1)
                    for j in range(2):
                        bank = dve_bank(("qk_sa", u, j))
                        for i in range(2):
                            t = 2 * j + i
                            last = nc.tensor.matmul(bank[:, 2 * D * i:2 * D * (i + 1)], hT[u][:, t * P:(t + 1) * P], w_sa[:, 0:2 * D],
                                                    start=True, stop=True)
                        last.then_inc(dve_filled, 1)
                    bank = act_bank(("v_sa", u))
                    nc.tensor.matmul(bank[:], w_sa[:, 2 * D:3 * D], hT[u][:], start=True, stop=True).then_inc(act_filled, 1)
                    yield
                    pe.wait_ge(act_emptied, act_item["v_sa", u] + 1)
                    bank = dve_bank(("sa_out", u))
                    for t in range(TILES):
                        last = nc.tensor.matmul(bank[:, t * D:(t + 1) * D], qT[u][:, 0, t * P:(t + 1) * P], w_sao[:],
                                                start=True, stop=True)
                    last.then_inc(dve_filled, 1)
                    yield
                    yield
                    transpose_norm(("hT_ca", u), LN_1, u)
                    yield
                    pe.wait_ge(act_emptied, act_item["hT_ca", u] + 1)
                    for c in range(2):
                        bank = act_bank(("q_ca", u, c))
                        nc.tensor.matmul(bank[:], w_caq[:, c, :], hT[u][:], start=True, stop=True).then_inc(act_filled, 1)
                    yield
                    yield from cross_attention_steps(u)
                    yield
                    transpose_norm(("hT_lin", u), LN_2, u)
                    yield
                    pe.wait_ge(act_emptied, act_item["hT_lin", u] + 1)
                    for m in range(FF // P):
                        bank = act_bank(("lin1", m, u))
                        nc.tensor.matmul(bank[:], w_l1[:, m * P:(m + 1) * P], hT[u][:], start=True, stop=True)\
                          .then_inc(act_filled, 1)
                    yield
                    pe.wait_ge(act_emptied, act_item["lin1", FF // P - 1, u] + 1)
                    bank = dve_bank(("lin2", u))
                    for t in range(TILES):
                        for m in range(FF // P):
                            last = nc.tensor.matmul(bank[:, t * D:(t + 1) * D], qT[u][:, m, t * P:(t + 1) * P], w_l2[:, m, :],
                                                    start=(m == 0), stop=(m == FF // P - 1))
                    last.then_inc(dve_filled, 1)
                    yield
                    yield
                    yield
                    yield

                    if u == 0:
                        pe.wait_ge(w_loaded["moe"], 6 * 16)
                    transpose_norm(("hT_moe", u), LN_MOE, u)
                    yield
                    pe.wait_ge(act_emptied, act_item["hT_moe", u] + 1)
                    bank = dve_bank(("logits", u))
                    for t in range(TILES):
                        last = nc.tensor.matmul(bank[:, t * EXPERTS:(t + 1) * EXPERTS], hT[u][:, t * P:(t + 1) * P], w_rt[:],
                                                start=True, stop=True)
                    last.then_inc(dve_filled, 1)
                    yield
                    yield
                    pe.wait_ge(cw_ready[u], 1)
                    bank = act_bank(("cwT", u))
                    for t in range(TILES):
                        last = nc.tensor.transpose(bank[0:EXPERTS, t * P:(t + 1) * P], cw[u][:, t, :], ident[:])
                    last.then_inc(act_filled, 1)
                    bank = dve_bank(("cwT_hm", u))[:, 0:SEQ // 2].bitcast(BF16)
                    for t in range(TILES):
                        last = nc.tensor.transpose(bank[:, t * P:(t + 1) * P], cw_hm[u][:, t, :], identb[:])
                    last.then_inc(dve_filled, 1)
                    bank = dve_bank(("cwT_lo", u))[:, 0:SEQ // 2].bitcast(BF16)
                    for t in range(TILES):
                        last = nc.tensor.transpose(bank[0:EXPERTS, t * P:(t + 1) * P], cw_lo[u][:, t, :], identb[:])
                    last.then_inc(dve_filled, 1)
                    yield
                    for c in range(CHUNKS + 2):
                        if c < CHUNKS:
                            expert_hidden(u, c)
                        if c >= 2:
                            expert_out(u, c - 2)
                        if c == CHUNKS + 1:
                            pe.wait_ge(act_emptied, act_item["cwT", u] + 1)
                            nc.tensor.matmul(moe_psum[:], b_m2[:], cwT[u], start=False, stop=True).then_inc(moe_filled, 1)
                        if c % PER_STEP == PER_STEP - 1:
                            yield
                    pe.wait_ge(moe_emptied, u + 1)
                    bank = dve_bank(("moe_out", u))
                    for t in range(TILES):
                        last = nc.tensor.transpose(bank[:, t * P:(t + 1) * P], qT[u][:, 0, t * P:(t + 1) * P], ident[:])
                    last.then_inc(dve_filled, 1)
                    yield

                in_turn(slot_steps)

            @block.scalar
            def _(act):
                taken = [0]

                def filled(name):
                    n = act_item[name]
                    assert n == taken[0], name
                    taken[0] += 1
                    act.wait_ge(act_filled, n + 1)
                    return act_psum[n % ACT_BANKS]

                def copy_bank(name, dst, bias=None, scale=1.0, n=P, w=SEQ):
                    bank = filled(name)
                    if bias is None:
                        nc.scalar.copy(dst, bank[0:n, 0:w]).then_inc(act_emptied, 1)
                    else:
                        nc.scalar.activation(dst, bank[0:n, 0:w], ACT.Identity, bias=bias, scale=scale).then_inc(act_emptied, 1)

                def exponentials(u, number, tiles, width, scale_of):
                    act.wait_ge(peak_ready[u], number + 1)
                    for i in range(tiles):
                        last = nc.scalar.activation(prob[u][:, i, 0:width], prob[u][:, i, 0:width], ACT.Exp,
                                                    bias=nbias[u][:, i:i + 1], scale=scale_of(i), accum_out=sums[u][:, i:i + 1])
                    last.then_inc(exp_done[u], 1)

                def exponentials_by_halves(u, number, width, scale_of):
                    for g in range(2):
                        act.wait_ge(peak_ready[u], half_done(number, g))
                        for i in range(HALF * g, HALF * g + HALF):
                            last = nc.scalar.activation(prob[u][:, i, 0:width], prob[u][:, i, 0:width], ACT.Exp,
                                                        bias=nbias[u][:, i:i + 1], scale=scale_of(i), accum_out=sums[u][:, i:i + 1])
                        last.then_inc(exp_done[u], 1)

                def local_attention_steps(l, u):
                    def take_qk(t):
                        if t > 0:
                            act.wait_ge(turned_ready[u], TILES * l + t)
                        for k in range(2):
                            copy_bank(("qk", l, t, u, k), raw[u][:, k, :])
                        act.wait_ge(act_emptied, act_item["qk", l, t, u, 1] + 1)
                        nc.scalar.activation(partner[u], raw[u], ACT.Square).then_inc(sq_ready[u], 1)

                    def take_v(j):
                        n = P if j < TILES else WINDOW
                        copy_bank(("v_loc", l, j, u), v_loc[u][0:n, j, :], n=n)

                    def take_turned(t, u):
                        bank = filled(("qT", l, t, u))
                        nc.scalar.copy(qT[u][:, :, t * P:(t + 1) * P], bank[:].rearrange("p (c q) -> p c q", q=P))\
                          .then_inc(act_emptied, 1)

                    def exp_local(t, u):
                        exponentials_by_halves(u, sm_local(l, t), KEYS, lambda i: rnorm[u][:, t, i:i + 1])

                    def take_ptb(t, u):
                        for g in range(2):
                            copy_bank(("ptb", l, t, u, g), ptb[u][0:WINDOW, 4 * g:4 * g + 4, :].rearrange("p t q -> p (t q)"), n=WINDOW)

                    def take_out(t, u):
                        copy_bank(("oT", l, t, u), hT[u][:])

                    for t in range(TILES):
                        take_qk(t)
                        if t >= 1:
                            take_turned(t - 1, u)
                        yield
                        take_v(t)
                        if t == TILES - 1:
                            take_v(TILES)
                        yield
                    take_turned(TILES - 1, u)
                    yield
                    for n in range(TILES + 1):
                        if n >= 1:
                            take_out(n - 1, u)
                        if n < TILES:
                            exp_local(n, u)
                        yield
                        if n < TILES:
                            take_ptb(n, u)
                        yield

                def cross_attention_steps(u):
                    def ca_exp(t, u):
                        exponentials_by_halves(u, sm_cross(t), CTX, lambda i: CA_DH ** -0.5)

                    def ca_take_ptb(t, u):
                        for g in range(2):
                            copy_bank(("ptb_ca", t, u, g), ptb[u][0:CH, 4 * g:4 * g + 4, :].rearrange("p t q -> p (t q)"), n=CH)

                    def ca_take_out(t, u):
                        copy_bank(("oT_ca", t, u), hT[u][:, 0:2 * P], w=2 * P)

                    for n in range(TILES + 1):
                        if n >= 1:
                            ca_take_out(n - 1, u)
                        if n < TILES:
                            ca_exp(n, u)
                        yield
                        if n < TILES:
                            ca_take_ptb(n, u)
                        yield

                def expert_hidden(u, c):
                    bank = filled(("moe_h", u, c))
                    if c < ROUTED:
                        if c >= 3:
                            act.wait_ge(dve_emptied, dve_item["moe_w", u, c - 3] + 1)
                        dst, bias = hid[u][:, c % 3, :], col("moe_b1", c)
                    else:
                        dst, bias = weighed[u][:, c % 3, :], col("sb1", c - ROUTED)
                    nc.scalar.activation(dst, bank[:], ACT.Silu, bias=bias).then_inc(act_emptied, 1)

                def slot_steps(u):
                    copy_bank(("ctxT", u), ctxT[u][:], w=CTX)
                    yield
                    copy_bank(("k", u), kcT[u][:, 0, :], bias=col("bk"), w=CTX)
                    yield
                    copy_bank(("hT_first", u), hT[u][:])
                    yield
                    copy_bank(("q", u), qT[u][:, 0, :], bias=col("bq"))
                    yield
                    exponentials(u, SM_FIRST, TILES, CTX, lambda i: D ** -0.5)
                    yield
                    copy_bank(("pt_first", u), ptb[u][0:CH, 0:TILES, :].rearrange("p t q -> p (t q)"), n=CH)
                    yield
                    yield
                    yield

                    for l in range(LAYERS):
                        bank = filled(("hTs", l, u))
                        nc.scalar.copy(hTs[u][0:D // 2, WINDOW:], bank[0:D // 2, :])
                        nc.scalar.copy(hTs[u][D // 2:D, WINDOW + 1:], bank[D // 2:D, 0:SEQ - 1]).then_inc(act_emptied, 1)
                        yield
                        yield from local_attention_steps(l, u)
                        yield
                        yield
                        copy_bank(("hT_ff", l, u), hT[u][:], bias=col("ln_b", l), scale=col("ln_g", l))
                        yield
                        for m, w in enumerate(HID_W):
                            bank = filled(("ff_g", l, m, u))
                            nc.scalar.activation(gel[u][0:w, m, :], bank[0:w, :], ACT.Gelu, bias=col("b1g", 3 * l + m, w))\
                              .then_inc(act_emptied, 1)
                        yield
                        yield

                    bank = filled(("kc", u))
                    for c in range(2):
                        last = nc.scalar.activation(kcT[u][:, c, :], bank[:, c * CTX:(c + 1) * CTX], ACT.Identity, bias=col("bk_ca", c))
                    last.then_inc(act_emptied, 1)
                    yield
                    copy_bank(("hT_sa", u), hT[u][:])
                    yield
                    copy_bank(("v_sa", u), qT[u][:, 0, :], bias=col("bv_sa"))
                    act.wait_ge(diag_ready[u], 1)
                    nc.scalar.activation(diag[u][:, 2, :], diag[u][:, 1, :], ACT.Exp, scale=float(D) ** 0.5).then_inc(diag_exp[u], 1)
                    yield
                    yield
                    yield
                    copy_bank(("hT_ca", u), hT[u][:], bias=col("ln1_b"), scale=col("ln1_g"))
                    yield
                    for c in range(2):
                        copy_bank(("q_ca", u, c), qT[u][:, c, :], bias=col("bq_ca", c))
                    yield
                    yield from cross_attention_steps(u)
                    yield
                    copy_bank(("hT_lin", u), hT[u][:], bias=col("ln2_b"), scale=col("ln2_g"))
                    yield
                    for m in range(FF // P):
                        bank = filled(("lin1", m, u))
                        nc.scalar.activation(qT[u][:, m, :], bank[:], ACT.Relu, bias=col("lin1_b", m)).then_inc(act_emptied, 1)
                    yield
                    yield
                    yield
                    yield
                    yield

                    copy_bank(("hT_moe", u), hT[u][:])
                    yield
                    act.wait_ge(logit_ready[u], 1)
                    nc.scalar.activation(expw[u], logit[u], ACT.Exp).then_inc(expw_ready[u], 1)
                    yield
                    yield
                    copy_bank(("cwT", u), cwT[u], n=EXPERTS)
                    yield
                    for c in range(CHUNKS + 2):
                        if c < CHUNKS:
                            expert_hidden(u, c)
                        if c == CHUNKS + 1:
                            act.wait_ge(moe_filled, u + 1)
                            nc.scalar.activation(qT[u][:, 0, :], moe_psum[:], ACT.Identity, bias=sb2_g[:], scale=gate[:, GF1:GF1 + 1])\
                              .then_inc(moe_emptied, 1)
                        if c % PER_STEP == PER_STEP - 1:
                            yield
                    yield

                in_turn(slot_steps)
                assert taken[0] == len(act_item)

            @block.vector
            def _(dve):
                taken = [0]
                links = [0]

                def filled(name):
                    n = dve_item[name]
                    assert n == taken[0], name
                    taken[0] += 1
                    dve.wait_ge(dve_filled, n + 1)
                    return dve_psum[n % DVE_BANKS]

                def link(ins):
                    links[0] += 1
                    ins.then_inc(dve_chain, 1)
                    dve.wait_ge(dve_chain, links[0])

                def norm_stats(src, u):
                    for t in range(TILES):
                        last = nc.vector.bn_stats(stats[u][:, t, :], src[u][:, t, :])
                    link(last)
                    for t in range(TILES):
                        last = nc.vector.bn_aggr(mv[u][:, t, :], stats[u][:, t, :])
                    last.then_inc(ln_stats[u], 1)

                def norm_apply(ln, src, dst, u):
                    dve.wait_ge(ln_rstd[u], ln + 1)
                    for t in range(TILES):
                        last = nc.vector.tensor_scalar(dst[u][:, t, :], src[u][:, t, :], mv[u][:, t, 0:1], rstd[u][:, t:t + 1],
                                                       ALU.subtract, ALU.mult)
                    last.then_inc(ln_done[u], 1)

                def divide(u, number, width):
                    for g in range(2):
                        some = slice(HALF * g, HALF * g + HALF)
                        dve.wait_ge(exp_done[u], half_done(number, g))
                        nc.vector.reciprocal(rinv[u][:, some], sums[u][:, some]).then_inc(rinv_ready[u], 1)
                    dve.wait_ge(rinv_ready[u], half_done(number, 1))
                    some = prob[u][:, HALF:, 0:width]
                    nc.vector.tensor_tensor(some, some, rinv[u][:, HALF:].unsqueeze(2).to_broadcast([P, HALF, width]),
                                            ALU.mult).then_inc(probs_hi_ready[u], 1)

                def mask_and_peak(bank, at, width, mask, u, i):
                    return nc.vector.tensor_tensor_reduce(out=prob[u][:, i, 0:width], in0=bank[:, at:at + width], in1=mask,
                                                          scale=1.0, scalar=LOWEST, op0=ALU.add, op1=ALU.max,
                                                          accum_out=peak[u][:, i:i + 1])

                def reciprocal_sums(u, number, n):
                    dve.wait_ge(exp_done[u], number + 1)
                    nc.vector.reciprocal(rinv[u][:, 0:n], sums[u][:, 0:n]).then_inc(rinv_ready[u], 1)

                def local_attention_steps(l, u):
                    def sum_squares(t, u):
                        dve.wait_ge(sq_ready[u], TILES * l + t + 1)
                        nc.vector.tensor_reduce(sumsq[u][:, t, :], partner[u].rearrange("p a (h d) -> p (a h) d", d=DH),
                                                AX.X, ALU.add).then_inc(sumsq_ready[u], 1)

                    def rotate_own(t, u):
                        heads = "p a (h d) -> p a h d"
                        nc.vector.tensor_tensor(turned[u].rearrange(heads, d=DH), raw[u].rearrange(heads, d=DH),
                                                tab_a[:, l, t, :, :].unsqueeze(2).to_broadcast([P, 2, HEADS, DH]), ALU.mult)\
                          .then_inc(own_ready[u], 1)

                    def add_partner(t, u):
                        dve.wait_ge(own_ready[u], TILES * l + t + 1)
                        dve.wait_ge(partner_ready[u], TILES * l + t + 1)
                        halves = "p a (h s d) -> p (a h) s d"
                        own, other = (v.rearrange(halves, s=2, d=DH // 2) for v in (turned[u], partner[u]))
                        nc.vector.tensor_tensor(own, own, other[:, :, ::-1, :], ALU.add).then_inc(turned_ready[u], 1)

                    def take_k(t, u):
                        bank = filled(("kT", l, t, u))
                        nc.vector.tensor_copy(kT[u][:, :, WINDOW + t * P:WINDOW + (t + 1) * P],
                                              bank[:].rearrange("p (c q) -> p c q", q=P)).then_inc(dve_emptied, 1)

                    def take_scores(t, u):
                        mask = masks[:, 0 if t == 0 else 1, :]
                        for g in range(2):
                            for odd in range(2):
                                bank = filled(("s_local", l, t, u, g, odd))
                                for i in range(2):
                                    last = mask_and_peak(bank, i * KEYS, KEYS, mask, u, 2 * (2 * g + i) + odd)
                                last.then_inc(dve_emptied, 1)
                            dve.wait_ge(dve_emptied, dve_item["s_local", l, t, u, g, 1] + 1)
                            if t == 0:
                                dve.wait_ge(rnorm_ready[u], TILES * (l + 1))
                            some = slice(HALF * g, HALF * g + HALF)
                            nc.vector.scalar_tensor_tensor(out=nbias[u][:, some], in0=peak[u][:, some], scalar=-1.0,
                                                           in1=rnorm[u][:, t, some], op0=ALU.mult, op1=ALU.mult)\
                              .then_inc(peak_ready[u], 1)

                    def take_pta(t, u):
                        for g in range(2):
                            bank = filled(("pta", l, t, u, g))
                            nc.vector.tensor_copy(pta[u][:, 4 * g:4 * g + 4, :].rearrange("p t q -> p (t q)"), bank[:])\
                              .then_inc(dve_emptied, 1)

                    def add_attention(t, u):
                        bank = filled(("attn_out", l, t, u))
                        nc.vector.tensor_tensor(y[u][:, t, :], bank[:, 0:D], y[u][:, t, :], ALU.add).then_inc(dve_emptied, 1)

                    for t in range(TILES):
                        if t >= 1:
                            take_k(t - 1, u)
                        sum_squares(t, u)
                        rotate_own(t, u)
                        yield
                        add_partner(t, u)
                        yield
                    take_k(TILES - 1, u)
                    yield
                    for n in range(TILES + 1):
                        if n < TILES:
                            take_scores(n, u)
                            divide(u, sm_local(l, n), KEYS)
                        yield
                        if n >= 1:
                            add_attention(n - 1, u)
                        if n < TILES:
                            take_pta(n, u)
                        yield

                def cross_attention_steps(u):
                    def ca_take_scores(t, u):
                        for g in range(2):
                            for j in (2 * g, 2 * g + 1):
                                bank = filled(("s_ca", t, u, j))
                                for c in range(2):
                                    last = mask_and_peak(bank, c * CTX, CTX, no_mask[:], u, 2 * j + c)
                                last.then_inc(dve_emptied, 1)
                            dve.wait_ge(dve_emptied, dve_item["s_ca", t, u, 2 * g + 1] + 1)
                            some = slice(HALF * g, HALF * g + HALF)
                            nc.vector.tensor_scalar(nbias[u][:, some], peak[u][:, some], -CA_DH ** -0.5, None, ALU.mult)\
                              .then_inc(peak_ready[u], 1)

                    def ca_take_pta(t, u):
                        for g in range(2):
                            bank = filled(("pta_ca", t, u, g))
                            nc.vector.tensor_copy(pta[u][0:CH, 4 * g:4 * g + 4, :].rearrange("p t q -> p (t q)"), bank[0:CH, :])\
                              .then_inc(dve_emptied, 1)

                    def ca_add(t, u):
                        if t == 0:
                            dve.wait_ge(res_ready[u], LAYERS + 2)
                        bank = filled(("ca_out", t, u))
                        nc.vector.tensor_tensor(y[u][:, t, :], bank[:, 0:D], res[u][:, t, :], ALU.add).then_inc(dve_emptied, 1)

                    for n in range(TILES + 1):
                        if n < TILES:
                            ca_take_scores(n, u)
                            divide(u, sm_cross(n), CTX)
                        yield
                        if n >= 1:
                            ca_add(n - 1, u)
                        if n < TILES:
                            ca_take_pta(n, u)
                            yield

                def route(u):
                    dve.wait_ge(expw_ready[u], 1)
                    for t in range(TILES):
                        last = nc.vector.max(top[u][:, t, :], expw[u][:, t, :])
                    link(last)
                    for t in range(TILES):
                        last = nc.vector.match_replace(rest[u][:, t, :], top[u][:, t, :], expw[u][:, t, :], 0.0)
                    link(last)
                    link(nc.vector.tensor_tensor(cw[u], expw[u], rest[u], ALU.subtract))
                    link(nc.vector.tensor_reduce(rsmall[u][:, 1, :], cw[u], AX.X, ALU.add))
                    link(nc.vector.reciprocal(rsmall[u][:, 2, :], rsmall[u][:, 1, :]))
                    link(nc.vector.tensor_tensor(cw[u], cw[u], rsmall[u][:, 2, :].unsqueeze(2).to_broadcast([P, TILES, EXPERTS]),
                                                 ALU.mult))
                    high, middle = cw_hm[u][:, :, 0:EXPERTS], cw_hm[u][:, :, EXPERTS:2 * EXPERTS]
                    link(nc.vector.tensor_copy(high, cw[u]))
                    link(nc.vector.tensor_tensor(rest[u], cw[u], high, ALU.subtract))
                    link(nc.vector.tensor_copy(middle, rest[u]))
                    nc.vector.tensor_tensor(cw_lo[u], rest[u], middle, ALU.subtract).then_inc(cw_ready[u], 1)

                def weigh(u, c):
                    bank = filled(("moe_w", u, c))
                    dve.wait_ge(act_emptied, act_item["moe_h", u, c] + 1)
                    nc.vector.tensor_tensor(weighed[u][:, c % 3, :], bank[:], hid[u][:, c % 3, :], ALU.mult).then_inc(dve_emptied, 1)

                def slot_steps(u):
                    dve.wait_ge(x_loaded[u], 16)
                    norm_stats(x, u)
                    yield
                    bank = filled(("v", u))
                    nc.vector.tensor_tensor(v_ctx[u][:, :, 0:D], bank[0:CH, 0:2 * D].rearrange("p (j n) -> p j n", j=2),
                                            row("bv", n=CH).unsqueeze(1).to_broadcast([CH, 2, D]), ALU.add).then_inc(dve_emptied, 1)
                    norm_apply(LN_XATTN, x, nrm, u)
                    yield
                    yield
                    yield
                    for t in range(TILES):
                        bank = filled(("s_first", u, t))
                        mask_and_peak(bank, 0, CTX, no_mask[:], u, t).then_inc(dve_emptied, 1)
                    dve.wait_ge(dve_emptied, dve_item["s_first", u, TILES - 1] + 1)
                    nc.vector.tensor_scalar(nbias[u][:, 0:TILES], peak[u][:, 0:TILES], -D ** -0.5, None, ALU.mult)\
                      .then_inc(peak_ready[u], 1)
                    yield
                    bank = filled(("pt_first", u))
                    nc.vector.tensor_copy(pta[u][0:CH, 0:TILES, :].rearrange("p t q -> p (t q)"), bank[0:CH, :]).then_inc(dve_emptied, 1)
                    reciprocal_sums(u, SM_FIRST, TILES)
                    dve.wait_ge(rinv_ready[u], SM_FIRST + 1)
                    link(nc.vector.tensor_scalar(rinv[u][:, 0:TILES], rinv[u][:, 0:TILES], gate[:, GX0:GX0 + 1], None, ALU.mult))
                    yield
                    bank = filled(("o_first", u))
                    for t in range(TILES):
                        last = nc.vector.scalar_tensor_tensor(out=x[u][:, t, :], in0=bank[:, t * D:(t + 1) * D],
                                                              scalar=rinv[u][:, t:t + 1], in1=x[u][:, t, :], op0=ALU.mult, op1=ALU.add)
                    last.then_inc(dve_emptied, 1)
                    dve.wait_ge(dve_emptied, dve_item["o_first", u] + 1)
                    norm_stats(x, u)
                    yield
                    norm_apply(LN_OUTER, x, y, u)
                    yield

                    for l in range(LAYERS):
                        yield
                        yield from local_attention_steps(l, u)
                        dve.wait_ge(shift_done[u], 4 * 16 * (l + 1))
                        norm_stats(shifted, u)
                        yield
                        norm_apply(LN_FF[l], shifted, nrm, u)
                        yield
                        yield
                        for m, w in enumerate(HID_W):
                            bank = filled(("ff_a", l, m, u))
                            dve.wait_ge(act_emptied, act_item["ff_g", l, m, u] + 1)
                            nc.vector.scalar_tensor_tensor(out=qT[u][0:w, m, :], in0=bank[0:w, :], scalar=col("b1a", 3 * l + m, w),
                                                           in1=gel[u][0:w, m, :], op0=ALU.add, op1=ALU.mult).then_inc(dve_emptied, 1)
                        yield
                        bank = filled(("ff_out", l, u))
                        dve.wait_ge(res_ready[u], l + 1)
                        nc.vector.tensor_tensor(flat(y[u]), bank[:], flat(res[u]), ALU.add).then_inc(dve_emptied, 1)
                        if l == LAYERS - 1:
                            dve.wait_ge(dve_emptied, dve_item["ff_out", l, u] + 1)
                            link(nc.vector.scalar_tensor_tensor(out=flat(x[u]), in0=flat(y[u]), scalar=gate[:, GF0:GF0 + 1],
                                                                in1=flat(x[u]), op0=ALU.mult, op1=ALU.add))
                            norm_stats(x, u)
                        yield

                    bank = filled(("vc", u))
                    nc.vector.tensor_tensor(v_ctx[u], bank[0:CH, :].rearrange("p (j n) -> p j n", j=2),
                                            row("bv_ca", 0, 2 * D, CH).unsqueeze(1).to_broadcast([CH, 2, 2 * D]), ALU.add).then_inc(dve_emptied, 1)
                    norm_apply(LN_TGT, x, y, u)
                    yield
                    yield
                    for j in range(2):
                        bank = filled(("qk_sa", u, j))
                        nc.vector.tensor_tensor(raw[u][:, j, :].rearrange("p (t n) -> p t n", t=2), bank[:].rearrange("p (t n) -> p t n", t=2),
                                                row("bqk_sa", 0, 2 * D).unsqueeze(1).to_broadcast([P, 2, 2 * D]), ALU.add)\
                          .then_inc(dve_emptied, 1)
                    dve.wait_ge(dve_emptied, dve_item["qk_sa", u, 1] + 1)
                    for t in range(TILES):
                        at = 2 * D * (t % 2)
                        last = nc.vector.tensor_tensor_reduce(out=partner[u][:, 0, t * D:(t + 1) * D], in0=raw[u][:, t // 2, at:at + D],
                                                              in1=raw[u][:, t // 2, at + D:at + 2 * D], scale=1.0, scalar=0.0,
                                                              op0=ALU.mult, op1=ALU.add, accum_out=diag[u][:, 0, t:t + 1])
                    link(last)
                    link(nc.vector.tensor_reduce(diag[u][:, 3, :], diag[u][:, 0, :].unsqueeze(2), AX.X, ALU.max))
                    nc.vector.tensor_tensor(diag[u][:, 1, :], diag[u][:, 0, :], diag[u][:, 3, :], ALU.subtract).then_inc(diag_ready[u], 1)
                    yield
                    dve.wait_ge(diag_exp[u], 1)
                    link(nc.vector.reciprocal(diag[u][:, 3, :], diag[u][:, 2, :]))
                    link(nc.vector.tensor_tensor(diag[u][:, 0, :], diag[u][:, 2, :], diag[u][:, 3, :], ALU.mult))
                    bank = filled(("sa_out", u))
                    dve.wait_ge(res_ready[u], LAYERS + 1)
                    for t in range(TILES):
                        last = nc.vector.scalar_tensor_tensor(out=y[u][:, t, :], in0=bank[:, t * D:(t + 1) * D],
                                                              scalar=diag[u][:, 0, t:t + 1], in1=res[u][:, t, :], op0=ALU.mult, op1=ALU.add)
                    last.then_inc(dve_emptied, 1)
                    dve.wait_ge(dve_emptied, dve_item["sa_out", u] + 1)
                    norm_stats(y, u)
                    yield
                    norm_apply(LN_1, y, nrm, u)
                    yield
                    yield
                    yield
                    yield from cross_attention_steps(u)
                    dve.wait_ge(dve_emptied, dve_item["ca_out", TILES - 1, u] + 1)
                    norm_stats(y, u)
                    yield
                    norm_apply(LN_2, y, nrm, u)
                    yield
                    yield
                    yield
                    bank = filled(("lin2", u))
                    dve.wait_ge(res_ready[u], LAYERS + 3)
                    nc.vector.tensor_tensor(flat(y[u]), bank[:], flat(res[u]), ALU.add).then_inc(dve_emptied, 1)
                    dve.wait_ge(dve_emptied, dve_item["lin2", u] + 1)
                    norm_stats(y, u)
                    yield
                    norm_apply(LN_3, y, nrm, u)
                    yield
                    dve.wait_ge(res_ready[u], LAYERS + 4)
                    link(nc.vector.tensor_tensor(flat(x[u]), flat(x[u]), flat(res[u]), ALU.add))
                    norm_stats(x, u)
                    yield
                    norm_apply(LN_MOE, x, nrm, u)
                    yield

                    yield
                    bank = filled(("logits", u))
                    nc.vector.tensor_tensor(logit[u], bank[:, 0:TILES * EXPERTS].rearrange("p (t e) -> p t e", t=TILES),
                                            row("router_b", 0, EXPERTS).unsqueeze(1).to_broadcast([P, TILES, EXPERTS]), ALU.add)\
                      .then_inc(dve_emptied, 1)
                    dve.wait_ge(dve_emptied, dve_item["logits", u] + 1)
                    link(nc.vector.tensor_reduce(rsmall[u][:, 0, :], logit[u], AX.X, ALU.max))
                    nc.vector.tensor_tensor(logit[u], logit[u], rsmall[u][:, 0, :].unsqueeze(2).to_broadcast([P, TILES, EXPERTS]),
                                            ALU.subtract).then_inc(logit_ready[u], 1)
                    yield
                    route(u)
                    yield
                    bank = filled(("cwT_hm", u))
                    nc.vector.tensor_copy(cwT_hm[u], bank[:, 0:SEQ // 2].bitcast(BF16)).then_inc(dve_emptied, 1)
                    bank = filled(("cwT_lo", u))
                    nc.vector.tensor_copy(cwT_lo[u], bank[0:EXPERTS, 0:SEQ // 2].bitcast(BF16)).then_inc(dve_emptied, 1)
                    yield
                    for c in range(CHUNKS + 2):
                        if c < ROUTED:
                            weigh(u, c)
                        if c % PER_STEP == PER_STEP - 1:
                            yield
                    bank = filled(("moe_out", u))
                    nc.vector.tensor_tensor(flat(y[u]), bank[:], flat(x[u]), ALU.add).then_inc(dve_emptied, 1)
                    yield

                in_turn(slot_steps)
                assert taken[0] == len(dve_item)

            @block.gpsimd
            def _(pool):
                links = [0]

                def link(ins):
                    links[0] += 1
                    ins.then_inc(pool_chain, 1)
                    pool.wait_ge(pool_chain, links[0])

                def norm_rstd(ln, u):
                    pool.wait_ge(ln_stats[u], ln + 1)
                    link(nc.gpsimd.tensor_scalar(rstd[u][:], mv[u][:, :, 1], EPS, None, ALU.add))
                    nc.gpsimd.tensor_tensor(rstd[u][:], rstd[u][:], neg_half[:, 0:TILES], ALU.pow).then_inc(ln_rstd[u], 1)

                def add_bias(u, bias):
                    nc.gpsimd.tensor_tensor(res[u][:], y[u][:], bias.unsqueeze(1).to_broadcast([P, TILES, D]), ALU.add)\
                      .then_inc(res_ready[u], 1)

                def scale_norm(ln, u, gain, bias):
                    pool.wait_ge(ln_done[u], ln + 1)
                    link(nc.gpsimd.tensor_tensor(res[u][:], nrm[u][:], gain.unsqueeze(1).to_broadcast([P, TILES, D]), ALU.mult))
                    nc.gpsimd.tensor_tensor(res[u][:], res[u][:], bias.unsqueeze(1).to_broadcast([P, TILES, D]), ALU.add)\
                      .then_inc(res_ready[u], 1)

                def divide(u, number, width):
                    pool.wait_ge(rinv_ready[u], half_done(number, 0))
                    some = prob[u][:, 0:HALF, 0:width]
                    nc.gpsimd.tensor_tensor(some, some, rinv[u][:, 0:HALF].unsqueeze(2).to_broadcast([P, HALF, width]), ALU.mult)\
                      .then_inc(probs_lo_ready[u], 1)

                def attention_steps(u, numbers, width):
                    for number in numbers:
                        divide(u, number, width)
                        yield
                        yield
                    yield

                def rest_for(steps):
                    for _ in range(steps):
                        yield

                def slot_steps(u):
                    norm_rstd(LN_XATTN, u)
                    yield
                    yield from rest_for(5)
                    norm_rstd(LN_OUTER, u)
                    yield
                    yield from rest_for(1)
                    for l in range(LAYERS):
                        def partners(t, u):
                            pool.wait_ge(sumsq_ready[u], TILES * l + t + 1)
                            heads = "p a (h d) -> p a h d"
                            nc.gpsimd.tensor_tensor(partner[u].rearrange(heads, d=DH), raw[u].rearrange(heads, d=DH),
                                                    tab_b[:, l, t, :, :].unsqueeze(2).to_broadcast([P, 2, HEADS, DH]), ALU.mult)\
                              .then_inc(partner_ready[u], 1)
                            link(nc.gpsimd.tensor_scalar(rnorm[u][:, t, :], sumsq[u][:, t, :], 1e-24, None, ALU.max))
                            nc.gpsimd.tensor_tensor(rnorm[u][:, t, :], rnorm[u][:, t, :], neg_half[:], ALU.pow).then_inc(rnorm_ready[u], 1)

                        def normalise_k(t, u):
                            pool.wait_ge(turned_ready[u], TILES * l + t + 1)
                            pool.wait_ge(rnorm_ready[u], TILES * l + t + 1)
                            k = turned[u][:, 1, :].rearrange("p (h d) -> p h d", d=DH)
                            nc.gpsimd.tensor_tensor(k, k, rnorm[u][:, t, HEADS:].unsqueeze(2).to_broadcast([P, HEADS, DH]), ALU.mult)\
                              .then_inc(k_ready[u], 1)

                        yield
                        for t in range(TILES):
                            partners(t, u)
                            yield
                            normalise_k(t, u)
                            yield
                        yield
                        yield from attention_steps(u, [sm_local(l, t) for t in range(TILES)], KEYS)
                        yield
                        pool.wait_ge(dve_emptied, dve_item["attn_out", l, TILES - 1, u] + 1)
                        add_bias(u, row("b2", l))
                        norm_rstd(LN_FF[l], u)
                        yield
                        yield from rest_for(3)
                        if l == LAYERS - 1:
                            norm_rstd(LN_TGT, u)
                        yield
                    pool.wait_ge(ln_done[u], LN_TGT + 1)
                    add_bias(u, row("sa_out_b"))
                    yield
                    yield from rest_for(2)
                    norm_rstd(LN_1, u)
                    yield
                    scale_norm(LN_1, u, row("ln1_g"), res1_b[:])
                    yield
                    yield from rest_for(2)
                    yield from attention_steps(u, [sm_cross(t) for t in range(TILES)], CTX)
                    norm_rstd(LN_2, u)
                    yield
                    scale_norm(LN_2, u, row("ln2_g"), res2_b[:])
                    yield
                    yield from rest_for(2)
                    norm_rstd(LN_3, u)
                    yield
                    scale_norm(LN_3, u, g3[:], b3[:])
                    yield
                    norm_rstd(LN_MOE, u)
                    yield
                    yield from rest_for(1 + 4 + (CHUNKS + 2) // PER_STEP + 1)

                in_turn(slot_steps)

            @block.sync
            def _(sp):
                def of_slot(dram, u):
                    return dram.rearrange("(i u) n d -> u i n d", u=len(SLOTS))[u][bass.ds(i_pass, 1)]

                for u in SLOTS:
                    sp.dma_start(ctx_t[u][:], of_slot(a["ctx"], u).rearrange("b (j p) d -> p (b j) d", p=CH))\
                      .then_inc(ctx_loaded[u], 16)
                    sp.dma_start(x[u][:], of_slot(a["x"], u).rearrange("b (t p) d -> p (b t) d", p=P))\
                      .then_inc(x_loaded[u], 16)
                half = D // 2
                for l in range(LAYERS):
                    for u in SLOTS:
                        sp.wait_ge(dve_emptied, dve_item["attn_out", l, TILES - 1, u] + 1)
                        sp.dma_start(shifted[u][:, :, 0:half], y[u][:, :, 0:half]).then_inc(shift_done[u], 16)
                        for lo, hi in ((0, 112), (112, P - 1)):
                            sp.dma_start(shifted[u][lo + 1:hi + 1, :, half:D], y[u][lo:hi, :, half:D]).then_inc(shift_done[u], 16)
                        sp.dma_start(shifted[u][0:1, 1:TILES, half:D], y[u][P - 1:P, 0:TILES - 1, half:D])\
                          .then_inc(shift_done[u], 16)
                for u in SLOTS:
                    sp.wait_ge(dve_emptied, dve_item["moe_out", u] + 1)
                    sp.dma_start(of_slot(out, u).rearrange("b (t p) d -> p (b t) d", p=P), y[u][:])\
                      .then_inc(x_stored[u], 16)
                for u in SLOTS:
                    sp.wait_ge(x_stored[u], 16)

        with nc.Fori(0, BATCH // len(SLOTS)) as i_pass:
            with nc.Block() as block:
                one_pass(i_pass, block)
            nc.all_engine_barrier(sems_to_clear=loop_sems)


def kernel(**inputs):
    import numpy as _np
    import concourse.bacc as _bacc
    from concourse import mybir as _mybir
    from ml_dtypes import bfloat16 as _bf16
    from concourse.bass_utils import run_bass_kernel_spmd as _run

    i = {k: _np.asarray(v) for k, v in inputs.items()}

    def column(*vs):
        out = []
        for v in vs:
            v = v.reshape(-1)
            n = -(-v.size // P) * P
            out.append(_np.concatenate([v, _np.zeros(n - v.size, v.dtype)]).reshape(-1, P).T)
        return _np.concatenate(out, 1)

    def spread(w):
        out = _np.zeros(w.shape[:-1] + (2, 4, 2 * CA_DH), w.dtype)
        out[..., :CA_DH] = _np.swapaxes(w.reshape(w.shape[:-1] + (4, 2, CA_DH)), -3, -2)
        return out.reshape(w.shape[:-1] + (2 * P,))

    in_w, in_b = i["L1_xattn_in_proj_w"], i["L1_xattn_in_proj_b"]
    b1 = i["L0_ffn_b1"]
    cols = {
        "bq": [i["L0_xattn_bq"]], "bk": [i["L0_xattn_bk"]], "ln_g": list(i["L0_ffn_ln_g"]), "ln_b": list(i["L0_ffn_ln_b"]),
        "b1a": [b1[l, :HID] for l in range(LAYERS)], "b1g": [b1[l, HID:] for l in range(LAYERS)],
        "bv_sa": [i["L1_xattn_qkv_b"][2 * D:]], "ln1_g": [i["L1_xattn_ln1_g"]], "ln1_b": [i["L1_xattn_ln1_b"]],
        "ln2_g": [i["L1_xattn_ln2_g"]], "ln2_b": [i["L1_xattn_ln2_b"]], "bq_ca": [spread(in_b[:D])],
        "bk_ca": [spread(in_b[D:2 * D])], "lin1_b": [i["L1_xattn_lin1_b"]], "moe_b1": [i["L1_ffn_b1"]],
        "sb1": [i["L1_ffn_sb1"]], "sb2": list(i["L1_ffn_sb2"])}
    rows = {
        "gates": _np.concatenate([i["g_xattn"], i["g_ffn"]]), "bv": i["L0_xattn_bv"], "qs": i["L0_ffn_q_scale"],
        "ks": i["L0_ffn_k_scale"], 
        "b2": i["L0_ffn_b2"], "bqk_sa": i["L1_xattn_qkv_b"][:2 * D], "sa_out_b": i["L1_xattn_sa_out_b"],
        "ln1_g": i["L1_xattn_ln1_g"], "ln1_b": i["L1_xattn_ln1_b"], "mha_out_b": i["L1_xattn_mha_out_b"],
        "ln2_g": i["L1_xattn_ln2_g"], "ln2_b": i["L1_xattn_ln2_b"], "lin2_b": i["L1_xattn_lin2_b"],
        "ln3_g": i["L1_xattn_ln3_g"], "ln3_b": i["L1_xattn_ln3_b"], "bv_ca": spread(in_b[2 * D:]),
        "router_b": i["L1_ffn_router_b"]}
    rot_a, rot_b = rotary_tables()
    arrays = {
        "x": i["x"], "ctx": i["ctx_1024"],
        "cols": _np.concatenate([column(*cols[n]) for n in COLS], 1),
        "rows": _np.concatenate([rows[n].reshape(-1) for n in ROWS])[None, :],
        "ident": _np.eye(P, dtype=_np.float32), "rot_a": rot_a, "rot_b": rot_b, "masks": band_masks(), 
        "sel": expert_selector().astype(_bf16), "identb": _np.eye(P).astype(_bf16),
        "wq": i["L0_xattn_Wq"], "wk": i["L0_xattn_Wk"], "wv": i["L0_xattn_Wv"],
        "wqkv": i["L0_ffn_wqkv"], "wo": i["L0_ffn_wo"], "w1": i["L0_ffn_w1"], "w2": i["L0_ffn_w2"],
        "w_sa": i["L1_xattn_qkv_w"].T, "w_sao": i["L1_xattn_sa_out_w"].T, "w_caq": spread(in_w[:D].T),
        "w_cak": spread(in_w[D:2 * D].T), "w_cav": spread(in_w[2 * D:].T),
        "w_cao": spread(i["L1_xattn_mha_out_w"]).reshape(D, 2, P).transpose(2, 1, 0),
        "w_l1": i["L1_xattn_lin1_w"].T, "w_l2": i["L1_xattn_lin2_w"].T, "w_rt": i["L1_ffn_router_w"],
        "w_m1": i["L1_ffn_w1"].transpose(1, 0, 2).reshape(D, EXPERTS * EXP_H), "b_m2": i["L1_ffn_b2"],
        "w_m2": i["L1_ffn_w2"].reshape(EXPERTS * EXP_H, D), "w_s1": i["L1_ffn_sw1"], "w_s2": i["L1_ffn_sw2"]}
    nc = _bacc.Bacc("TRN2", target_bir_lowering=False, num_devices=1)
    aps, fed = {}, {}
    for name, v in arrays.items():
        v = _np.ascontiguousarray(v)
        fed[f"in_{name}_dram"] = v
        aps[name] = nc.dram_tensor(f"in_{name}_dram", v.shape, _mybir.dt.from_np(v.dtype), kind="ExternalInput").ap()
    out = nc.dram_tensor("out_0_dram", (BATCH, SEQ, D), _mybir.dt.float32, kind="ExternalOutput").ap()
    build(nc, aps, out)
    r = _run(nc, [fed], core_ids=[0])
    return r.results[0]["out_0_dram"]
```
